# Optimizing a Trainium2 kernel written in Bass

```python
import numpy as np
import jax
import jax.numpy as jnp

def _softmax(x, axis=-1):
    return jax.nn.softmax(x, axis=axis)

def _gelu(x):
    return jax.nn.gelu(x, approximate=True)

def _silu(x):
    return jax.nn.silu(x)

def _sigmoid(x):
    return jax.nn.sigmoid(x)

def _layernorm(x, axis=-1, eps=1e-05):
    m = jnp.mean(x, axis=axis, keepdims=True)
    v = jnp.var(x, axis=axis, keepdims=True)
    return (x - m) / jnp.sqrt(v + eps)

def _scatter_add(tgt, idx, src, axis=0):
    return tgt.at[idx].add(src)

def _segment_sum(src, seg, n):
    return jax.ops.segment_sum(src, seg, n)
kernel_name = 'mk_gnn_preln_d1_gnn_r32_b35723'

def setup_inputs(seed: int=0):
    np.random.seed(seed)
    _w = jnp.asarray

    def _rec_inputs():
        import jax
        import jax.numpy as jnp
        _gk = jax.random.key(seed)
        x = -0.0006008 + 1.001 * jax.random.normal(jax.random.fold_in(_gk, 1), (3125, 128), jnp.float32)
        src = jax.random.randint(jax.random.fold_in(_gk, 2), (50000,), 0, 3125, jnp.int32)
        dst = jax.random.randint(jax.random.fold_in(_gk, 3), (50000,), 0, 3125, jnp.int32)
        _o = jnp.argsort(dst, stable=True)
        src = src[_o]
        dst = dst[_o]
        edge_type_4 = jax.random.randint(jax.random.fold_in(_gk, 12), (50000,), 0, 4, jnp.int32)
        edge_weight = jax.random.uniform(jax.random.fold_in(_gk, 13), (50000,), jnp.float32, 0.0, 0.999996)
        return (x, src, dst, edge_type_4, edge_weight)
    x, src, dst, edge_type_4, edge_weight = _rec_inputs()

    def _L0_gnn_setup():
        import jax, jax.numpy as jnp
        import numpy as np
        NUM_RELATIONS = 4
        N_NODES = 625
        N_EDGES = 10000
        F_IN = 128
        HID = 128
        EMB = 128

        def _rgcn_conv(x, src, dst, edge_type, edge_weight, W, root, bias):
            xj = x[src]
            m = jnp.zeros((xj.shape[0], W.shape[2]), dtype=x.dtype)
            for r in range(W.shape[0]):
                mask = (edge_type == r).astype(x.dtype)[:, None]
                m = m + mask * (xj @ W[r])
            m = m * edge_weight[:, None]
            out = jax.ops.segment_sum(m, dst, num_segments=x.shape[0])
            return out + x @ root + bias
        key = jax.random.key(seed)
        ks = jax.random.split(key, 10)
        return {'x': jax.random.normal(ks[0], (N_NODES, F_IN), dtype=jnp.float32), 'edge_index': jax.random.randint(ks[1], (2, N_EDGES), 0, N_NODES, dtype=jnp.int64 if jax.config.jax_enable_x64 else jnp.int32).astype(jnp.int32), 'edge_type': jax.random.randint(ks[2], (N_EDGES,), 0, NUM_RELATIONS).astype(jnp.int32), 'edge_weight': jax.random.uniform(ks[3], (N_EDGES,), dtype=jnp.float32), 'W1': jax.random.normal(ks[4], (NUM_RELATIONS, F_IN, HID), dtype=jnp.float32) * 0.05, 'root1': jax.random.normal(ks[5], (F_IN, HID), dtype=jnp.float32) * 0.05, 'b1': jax.random.normal(ks[6], (HID,), dtype=jnp.float32) * 0.05, 'W2': jax.random.normal(ks[7], (NUM_RELATIONS, HID, EMB), dtype=jnp.float32) * 0.05, 'root2': jax.random.normal(ks[8], (HID, EMB), dtype=jnp.float32) * 0.05, 'b2': jax.random.normal(ks[9], (EMB,), dtype=jnp.float32) * 0.05}
    _L0_gnn_all = _L0_gnn_setup()
    _L0_gnn_in = {k: v for k, v in _L0_gnn_all.items() if k in ('W1', 'root1', 'b1', 'W2', 'root2', 'b2')}
    del _L0_gnn_all
    return {'x': x, 'src': src, 'dst': dst, 'edge_type_4': edge_type_4, 'edge_weight': edge_weight, 'L0_gnn_W1': _L0_gnn_in['W1'], 'L0_gnn_root1': _L0_gnn_in['root1'], 'L0_gnn_b1': _L0_gnn_in['b1'], 'L0_gnn_W2': _L0_gnn_in['W2'], 'L0_gnn_root2': _L0_gnn_in['root2'], 'L0_gnn_b2': _L0_gnn_in['b2']}

def reference(x, src, dst, edge_type_4, edge_weight, L0_gnn_W1, L0_gnn_root1, L0_gnn_b1, L0_gnn_W2, L0_gnn_root2, L0_gnn_b2):
    import jax
    import jax.numpy as jnp

    def _L0_gnn_ref(x, edge_index, edge_type, edge_weight, W1, root1, b1, W2, root2, b2):
        import jax, jax.numpy as jnp
        import numpy as np
        NUM_RELATIONS = 4
        N_NODES = 625
        N_EDGES = 10000
        F_IN = 128
        HID = 128
        EMB = 128

        def _rgcn_conv(x, src, dst, edge_type, edge_weight, W, root, bias):
            xj = x[src]
            m = jnp.zeros((xj.shape[0], W.shape[2]), dtype=x.dtype)
            for r in range(W.shape[0]):
                mask = (edge_type == r).astype(x.dtype)[:, None]
                m = m + mask * (xj @ W[r])
            m = m * edge_weight[:, None]
            out = jax.ops.segment_sum(m, dst, num_segments=x.shape[0])
            return out + x @ root + bias
        src, dst = (edge_index[0], edge_index[1])
        ew = (edge_weight - edge_weight.min()) / (edge_weight.max() - edge_weight.min() + 1e-08)
        h = jax.nn.relu(_rgcn_conv(x, src, dst, edge_type, ew, W1, root1, b1))
        h = _rgcn_conv(h, src, dst, edge_type, ew, W2, root2, b2)
        return h
    edge_index = jnp.stack([src, dst])
    h = jnp.maximum(_layernorm(x, axis=-1), 0.0)
    x = x + _L0_gnn_ref(h, edge_index, edge_type_4, edge_weight, L0_gnn_W1, L0_gnn_root1, L0_gnn_b1, L0_gnn_W2, L0_gnn_root2, L0_gnn_b2)
    return x

_drawn_inputs = setup_inputs


def setup_inputs(seed=0):
    import zlib

    import numpy as np

    out = dict(_drawn_inputs(seed))
    spreads = {}
    factors = {}
    for name, (base, spread) in spreads.items():
        noise = np.random.default_rng([zlib.crc32(name.encode()), seed]).standard_normal(out[name].shape)
        drawn = base * np.exp(spread * noise) if base else spread * noise
        out[name] = jnp.asarray(drawn.astype(out[name].dtype))
    for name, factor in factors.items():
        out[name] = (out[name] * factor).astype(out[name].dtype)
    return out
```

```python
import concourse.bass as bass
from concourse import mybir
from contextlib import ExitStack

P = 128
N_NODES = 3125
N_EDGES = 50000
F = 128
R = 4
BLOCKS = -(-N_NODES // P)
NODES = BLOCKS * P
GROUP = 4
TILES = -(-N_EDGES // (P * GROUP)) * GROUP
GROUPS = TILES // GROUP
WINDOW = 64
SLOTS = 4


def gnn_kernel(nc, x_rows, x_cols, src, dst, group_base, edge_type, edge_weight,
               W1, root1, b1, W2, root2, b2, out_cols):
    fp32 = mybir.dt.float32
    i32 = mybir.dt.int32
    ALU = mybir.AluOpType
    ACT = mybir.ActivationFunctionType
    AX = mybir.AxisListType
    ds = bass.ds

    ctx = ExitStack()
    with ctx:
        def sb(name, shape, dt=fp32):
            return ctx.enter_context(nc.sbuf_tensor(name, shape, dt))

        def ps(name, shape):
            return ctx.enter_context(nc.psum_tensor(name, shape, fp32))

        def sem(name):
            return ctx.enter_context(nc.semaphore(name))

        table = [nc.dram_tensor(f"message_rows{l}", [NODES * R, F], fp32, kind="Internal").ap() for l in range(2)]
        x_sb = sb("x_sb", [P, BLOCKS * F])
        xT_sb = sb("xT_sb", [P, NODES])
        W_sb = [sb(f"W_sb{l}", [P, R * F]) for l in range(2)]
        root_sb = [sb(f"root_sb{l}", [P, F]) for l in range(2)]
        b_sb = [sb(f"b_sb{l}", [P, 1]) for l in range(2)]
        src_sb = sb("src_sb", [P, TILES], i32)
        type_sb = sb("type_sb", [P, TILES], i32)
        dst_sb = sb("dst_sb", [P, TILES], i32)
        base_sb = sb("base_sb", [P, GROUPS], i32)
        ew_sb = sb("ew_sb", [P, TILES])
        row_index = sb("row_index", [P, TILES], i32)
        weight = sb("weight", [P, TILES])
        rel = sb("rel", [P, TILES])
        inside = sb("inside", [P, TILES])
        stray_dst = sb("stray_dst", [P, TILES])
        extremes = sb("extremes", [P, 3])
        extremes_all = sb("extremes_all", [P, 3])
        stray_flag = sb("stray_flag", [P, 1], i32)
        inv_range = sb("inv_range", [P, 2])
        stats = sb("stats", [P, BLOCKS, 6])
        moments = sb("moments", [P, BLOCKS, 2])
        rstd = sb("rstd", [P, BLOCKS])
        shift = sb("shift", [P, BLOCKS])
        eps = sb("eps", [P, 1])
        columns = sb("columns", [P, P])
        identity = sb("identity", [P, P])
        h_rows = sb("h_rows", [P, SLOTS, F])
        h_cols = sb("h_cols", [P, SLOTS, P])
        y_stage = sb("y_stage", [P, SLOTS, R * F])
        sums = [sb(f"sums{l}", [P, NODES]) for l in range(2)]
        select = sb("select", [P, TILES * WINDOW])
        gathered = sb("gathered", [P, SLOTS, GROUP, F])
        stray_select = sb("stray_select", [P, P])
        stray_rel = sb("stray_rel", [P, 1])
        slot_index = sb("slot_index", [P, SLOTS, GROUP], i32)
        stray_index = sb("stray_index", [P, 1], i32)

        y_ps = [ps(f"y_ps{k}", [P, R * F]) for k in range(2)]
        t_ps = [ps(f"t_ps{k}", [P, 512]) for k in range(2)]
        r_ps = [ps(f"r_ps{k}", [P, 512]) for k in range(2)]
        win_ps = [ps(f"win_ps{k}", [P, 512]) for k in range(2)]

        x_loaded = [sem(f"x_loaded{c}") for c in range(5)]
        edges_loaded = sem("edges_loaded")
        params_loaded = sem("params_loaded")
        xT_loaded = sem("xT_loaded")
        constants_ready = sem("constants_ready")
        identity_ready = sem("identity_ready")
        dve_step = sem("dve_step")
        moments_ready = sem("moments_ready")
        rstd_ready = sem("rstd_ready")
        norm_ready = sem("norm_ready")
        extremes_ready = sem("extremes_ready")
        extremes_reduced = sem("extremes_reduced")
        weights_scaled = sem("weights_scaled")
        weights_ready = sem("weights_ready")
        index_ready = sem("index_ready")
        flag_ready = sem("flag_ready")
        h_rows_ready = sem("h_rows_ready")
        transposed = sem("transposed")
        h_cols_ready = [sem(f"h_cols_ready{l}") for l in range(2)]
        y_multiplied = [sem(f"y_multiplied{l}") for l in range(2)]
        y_staged = [sem(f"y_staged{l}") for l in range(2)]
        root_added = [sem(f"root_added{l}") for l in range(2)]
        y_stored = [[sem(f"y_stored{l}_{s}") for s in range(SLOTS)] for l in range(2)]
        rows_gathered = [[sem(f"rows_gathered{l}_{s}") for s in range(SLOTS)] for l in range(2)]
        slot_indexed = [sem(f"slot_indexed{l}") for l in range(2)]
        gathers_begun = sem("gathers_begun")
        select_ready = sem("select_ready")
        stray_indexed = sem("stray_indexed")
        stray_moved = sem("stray_moved")
        window_summed = [sem(f"window_summed{l}") for l in range(2)]
        window_added = [sem(f"window_added{l}") for l in range(2)]
        stray_gathered = sem("stray_gathered")
        stray_selected = sem("stray_selected")
        stray_summed = sem("stray_summed")
        stray_added = sem("stray_added")
        layer_done = [sem(f"layer_done{l}") for l in range(2)]
        out_stored = sem("out_stored")

        LAPS = BLOCKS // SLOTS - 1

        def over_blocks(eng, step):
            for b in range(SLOTS):
                step(b, b, 0)
            with eng.Fori(1, LAPS) as lap:
                for s in range(SLOTS):
                    step(lap * SLOTS + s, s, lap)
            for b in range(LAPS * SLOTS, BLOCKS):
                step(b, b % SLOTS, b // SLOTS)

        GLAPS = GROUPS // SLOTS

        def over_groups(eng, step):
            for g in range(SLOTS):
                step(g, g, 0)
            with eng.Fori(1, GLAPS) as lap:
                for s in range(SLOTS):
                    step(lap * SLOTS + s, s, lap)
            for g in range(GLAPS * SLOTS, GROUPS):
                step(g, g % SLOTS, g // SLOTS)

        def past(k, n):
            return not isinstance(k, int) or k >= n

        def exists(k, n):
            return not isinstance(k, int) or k < n

        block = ctx.enter_context(nc.Block())

        @block.sync
        def _(sp):
            per = BLOCKS // 5
            for c in range(5):
                sp.dma_start(x_sb[:, c * per * F:(c + 1) * per * F].rearrange("p (b f) -> p b f", f=F),
                             x_rows[c * per * P:(c + 1) * per * P, :].rearrange("(b p) f -> p b f", p=P)
                             ).then_inc(x_loaded[c], 16)
            sp.dma_start(xT_sb[:, :], x_cols).then_inc(xT_loaded, 16)
            for l in range(2):
                y_view = table[l].rearrange("(n r) f -> n (r f)", r=R)

                def store(b, s, lap):
                    sp.wait_ge(y_staged[l], b + 1)
                    sp.dma_start(y_view[ds(b * P, P), :], y_stage[:, s, :]).then_inc(y_stored[l][s], 16)
                over_blocks(sp, store)
            sp.wait_ge(layer_done[1], 1)
            sp.dma_start(out_cols, sums[1][:, :]).then_inc(out_stored, 16)
            sp.wait_ge(out_stored, 16)

        @block.gpsimd
        def _(pool):
            nc.gpsimd.iota(columns[:, :], pattern=[[1, P]], base=0, channel_multiplier=0,
                           allow_small_or_imprecise_dtypes=True).then_inc(constants_ready, 1)
            nc.gpsimd.memset(eps[:, :], 1e-5).then_inc(constants_ready, 1)
            nc.gpsimd.memset(identity[:, :], 0.0).then_inc(identity_ready, 1)
            pool.wait_ge(identity_ready, 1)
            nc.gpsimd.affine_select(out=identity[:, :], in_=identity[:, :], compare_op=ALU.not_equal, fill=1.0,
                                    base=0, pattern=[[-1, P]], channel_multiplier=1).then_inc(identity_ready, 1)
            pool.wait_ge(extremes_ready, 1)
            nc.gpsimd.partition_all_reduce(extremes_all[:, :], extremes[:, :], P,
                                           bass.bass_isa.ReduceOp.max).then_inc(extremes_reduced, 1)
            pool.wait_ge(weights_scaled, 1)
            tail = N_EDGES // P
            nc.gpsimd.affine_select(out=weight[:, tail:], in_=weight[:, tail:], compare_op=ALU.is_ge, fill=0.0,
                                    base=N_EDGES - 1 - tail * P, pattern=[[-P, TILES - tail]],
                                    channel_multiplier=-1).then_inc(weights_ready, 1)
            for l in range(2):
                for s in range(SLOTS):
                    pool.wait_ge(y_stored[l][s], 16 * len(range(s, BLOCKS, SLOTS)))

                def gather(g, s, lap):
                    pool.wait_ge(slot_indexed[l], g + 1)
                    pool.sem_inc(gathers_begun, 1)
                    for k in range(GROUP):
                        nc.gpsimd.indirect_dma_start(
                            out=gathered[:, s, k, :], out_offset=None, in_=table[l],
                            in_offset=bass.IndirectOffsetOnAxis(ap=slot_index[:, s, k:k + 1], axis=0),
                        ).then_inc(rows_gathered[l][s], 16)
                over_groups(pool, gather)
                pool.wait_ge(window_summed[l], GROUPS)
                pool.wait_ge(flag_ready, 1)
                strays = pool.value_load(stray_flag[0:1, 0:1], min_val=0, max_val=1)
                with pool.If(strays != 0):
                    with pool.Fori(0, TILES) as t:
                        pool.wait_ge(stray_indexed, t + l * TILES + 1)
                        pool.sem_inc(gathers_begun, 1)
                        nc.gpsimd.indirect_dma_start(
                            out=gathered[:, 0, 0, :], out_offset=None, in_=table[l],
                            in_offset=bass.IndirectOffsetOnAxis(ap=stray_index[:, :], axis=0),
                        ).then_inc(stray_gathered, 16)

        @block.scalar
        def _(act):
            act.dma_start(W_sb[0][:, :], W1).then_inc(params_loaded, 16)
            act.dma_start(root_sb[0][:, :], root1).then_inc(params_loaded, 16)
            act.dma_start(b_sb[0][:, :], b1).then_inc(params_loaded, 16)
            act.dma_start(dst_sb[:, :], dst).then_inc(edges_loaded, 16)
            act.dma_start(base_sb[:, :], group_base.partition_broadcast(P)).then_inc(edges_loaded, 16)
            act.dma_start(ew_sb[:, :], edge_weight).then_inc(edges_loaded, 16)
            act.dma_start(src_sb[:, :], src).then_inc(edges_loaded, 16)
            act.dma_start(type_sb[:, :], edge_type).then_inc(edges_loaded, 16)
            act.dma_start(W_sb[1][:, :], W2).then_inc(params_loaded, 16)
            act.dma_start(root_sb[1][:, :], root2).then_inc(params_loaded, 16)
            act.dma_start(b_sb[1][:, :], b2).then_inc(params_loaded, 16)
            act.wait_ge(constants_ready, 2)
            act.wait_ge(moments_ready, 1)
            nc.scalar.activation(rstd[:, :], moments[:, :, 1], ACT.Sqrt, bias=eps[:, :]).then_inc(rstd_ready, 1)
            act.wait_ge(norm_ready, 1)

            def normalise(b, s):
                if past(b, SLOTS):
                    act.wait_ge(transposed, b - SLOTS + 1)
                nc.scalar.activation(h_rows[:, s, :], x_sb[:, ds(b * F, F)], ACT.Relu,
                                     bias=shift[:, ds(b, 1)], scale=rstd[:, ds(b, 1)]).then_inc(h_rows_ready, 1)

            for l in range(2):
                if l == 0:
                    normalise(0, 0)
                    normalise(1, 1)

                def step(b, s, lap):
                    if l == 0 and exists(b + 2, BLOCKS):
                        normalise(b + 2, (s + 2) % SLOTS)
                    act.wait_ge(y_multiplied[l], b + 1)
                    if past(b, SLOTS):
                        act.wait_ge(y_stored[l][s], 16 * lap)
                    nc.scalar.copy(y_stage[:, s, :], y_ps[s % 2][:, :]).then_inc(y_staged[l], 1)
                over_blocks(act, step)
                act.wait_ge(index_ready, 1)

                def place_index(g, s, lap):
                    if past(g, SLOTS):
                        act.wait_ge(window_summed[l], g - SLOTS + 1)
                    nc.scalar.copy(slot_index[:, s, :], row_index[:, ds(g * GROUP, GROUP)]
                                   ).then_inc(slot_indexed[l], 1)
                over_groups(act, place_index)

        @block.vector
        def _(dve):
            steps = [0]

            def link(instruction):
                steps[0] += 1
                instruction.then_inc(dve_step, 1)
                dve.wait_ge(dve_step, steps[0])

            for c in range(5):
                dve.wait_ge(x_loaded[c], 16)
                for b in range(c * 5, c * 5 + 5):
                    last = nc.vector.bn_stats(stats[:, b, :], x_sb[:, b * F:(b + 1) * F])
            link(last)
            for b in range(BLOCKS):
                last = nc.vector.bn_aggr(moments[:, b, :], stats[:, b, :])
            last.then_inc(moments_ready, 1)
            dve.wait_ge(rstd_ready, 1)
            link(nc.vector.reciprocal(rstd[:, :], rstd[:, :]))
            nc.vector.scalar_tensor_tensor(out=shift[:, :], in0=moments[:, :, 0], scalar=-1.0, in1=rstd[:, :],
                                           op0=ALU.mult, op1=ALU.mult).then_inc(norm_ready, 1)

            def take_transposed(b, s):
                dve.wait_ge(transposed, b + 1)
                if past(b, SLOTS):
                    dve.wait_ge(y_multiplied[0], b - SLOTS + 1)
                nc.vector.tensor_copy(h_cols[:, s, :], t_ps[s % 2][:, 0:P]).then_inc(h_cols_ready[0], 1)

            def relu(b, s):
                if past(b, SLOTS):
                    dve.wait_ge(y_multiplied[1], b - SLOTS + 1)
                nc.vector.tensor_scalar(h_cols[:, s, :], sums[0][:, ds(b * P, P)], 0.0, None, ALU.max
                                        ).then_inc(h_cols_ready[1], 1)

            def table_stage(l):
                dve.wait_ge(params_loaded, 96)
                columns_of_h = take_transposed if l == 0 else relu
                columns_of_h(0, 0)
                if l == 1:
                    dve.wait_ge(xT_loaded, 16)

                def step(b, s, lap):
                    if exists(b + 1, BLOCKS):
                        columns_of_h(b + 1, (s + 1) % SLOTS)
                    dve.wait_ge(y_multiplied[l], b + 1)
                    if l == 0:
                        nc.vector.tensor_scalar(sums[0][:, ds(b * P, P)], r_ps[s % 2][:, 0:P], b_sb[0][:, :], None,
                                                ALU.add).then_inc(root_added[0], 1)
                    else:
                        nc.vector.scalar_tensor_tensor(out=sums[1][:, ds(b * P, P)], in0=r_ps[s % 2][:, 0:P],
                                                       scalar=b_sb[1][:, :], in1=xT_sb[:, ds(b * P, P)],
                                                       op0=ALU.add, op1=ALU.add).then_inc(root_added[1], 1)
                over_blocks(dve, step)

            def edge_preparation():
                dve.wait_ge(edges_loaded, 80)
                nc.vector.scalar_tensor_tensor(out=row_index[:, :], in0=src_sb[:, :], scalar=float(R),
                                               in1=type_sb[:, :], op0=ALU.mult, op1=ALU.add).then_inc(index_ready, 1)
                nc.vector.tensor_reduce(out=extremes[:, 0:1], in_=ew_sb[:, :], axis=AX.X, op=ALU.max)
                nc.vector.tensor_reduce(out=extremes[:, 1:2], in_=ew_sb[:, :], axis=AX.X, op=ALU.min, negate=True)
                link(nc.vector.tensor_tensor(rel[:, :].rearrange("p (g k) -> p g k", k=GROUP),
                                             dst_sb[:, :].rearrange("p (g k) -> p g k", k=GROUP),
                                             base_sb[:, :, None].to_broadcast([P, GROUPS, GROUP]), ALU.subtract))
                link(nc.vector.tensor_scalar(inside[:, :], rel[:, :], 0.0, None, ALU.is_ge))
                link(nc.vector.scalar_tensor_tensor(out=inside[:, :], in0=rel[:, :], scalar=float(WINDOW),
                                                    in1=inside[:, :], op0=ALU.is_lt, op1=ALU.mult))
                link(nc.vector.tensor_reduce(out=inv_range[:, 0:1], in_=inside[:, :], axis=AX.X, op=ALU.min))
                nc.vector.tensor_scalar(extremes[:, 2:3], inv_range[:, 0:1], -1.0, 1.0, ALU.mult, ALU.add
                                        ).then_inc(extremes_ready, 1)
                link(nc.vector.scalar_tensor_tensor(out=stray_dst[:, :], in0=inside[:, :], scalar=-65536.0,
                                                    in1=dst_sb[:, :], op0=ALU.mult, op1=ALU.add))
                dve.wait_ge(extremes_reduced, 1)
                nc.vector.tensor_copy(stray_flag[:, :], extremes_all[:, 2:3]).then_inc(flag_ready, 1)
                link(nc.vector.tensor_scalar(inv_range[:, 0:1], extremes_all[:, 0:1], extremes_all[:, 1:2], 1e-8,
                                             ALU.add, ALU.add))
                link(nc.vector.reciprocal(inv_range[:, 1:2], inv_range[:, 0:1]))
                nc.vector.tensor_scalar(weight[:, :], ew_sb[:, :], extremes_all[:, 1:2], inv_range[:, 1:2],
                                        ALU.add, ALU.mult).then_inc(weights_scaled, 1)
                dve.wait_ge(weights_ready, 1)
                dve.wait_ge(constants_ready, 2)

            AHEAD = 4

            def build_select(g):
                for k in range(GROUP):
                    t = g * GROUP + k
                    last = nc.vector.tensor_scalar(select[:, ds(t * WINDOW, WINDOW)], columns[:, 0:WINDOW],
                                                   rel[:, ds(t, 1)], weight[:, ds(t, 1)],
                                                   ALU.is_equal, ALU.mult)
                last.then_inc(select_ready, 1)

            def edge_stage(l):
                if l == 0:
                    for g in range(AHEAD):
                        build_select(g)

                def step(g, s, lap):
                    if l == 0 and exists(g + AHEAD, GROUPS):
                        build_select(g + AHEAD)
                    base = dve.value_load(base_sb[0:1, ds(g, 1)], min_val=0, max_val=N_NODES - 1)
                    dve.wait_ge(window_summed[l], g + 1)
                    if past(g, 1):
                        dve.wait_ge(window_added[l], g)
                    nc.vector.tensor_tensor(sums[l][:, ds(base, WINDOW)], sums[l][:, ds(base, WINDOW)],
                                            win_ps[s % 2][:, 0:WINDOW], ALU.add).then_inc(window_added[l], 1)
                if l == 0:
                    for g in range(SLOTS):
                        step(g, g, 0)
                    with dve.Fori(1, GLAPS - 1) as lap:
                        for s in range(SLOTS):
                            step(lap * SLOTS + s, s, lap)
                    for g in range((GLAPS - 1) * SLOTS, GROUPS):
                        step(g, g % SLOTS, g // SLOTS)
                else:
                    over_groups(dve, step)
                dve.wait_ge(window_added[l], GROUPS)

            def stray_stage(l):
                strays = dve.value_load(stray_flag[0:1, 0:1], min_val=0, max_val=1)
                with dve.If(strays != 0):
                    with dve.Fori(0, TILES) as t:
                        done = (t + l * TILES) * BLOCKS
                        nc.vector.tensor_copy(stray_index[:, :], row_index[:, ds(t, 1)]).then_inc(stray_indexed, 1)
                        nc.vector.tensor_copy(stray_rel[:, :], stray_dst[:, ds(t, 1)]).then_inc(stray_moved, 1)
                        with dve.Fori(0, BLOCKS) as b:
                            dve.wait_ge(stray_moved, done + t + l * TILES + b + 1)
                            nc.vector.tensor_scalar(stray_select[:, :], columns[:, :], stray_rel[:, :],
                                                    weight[:, ds(t, 1)], ALU.is_equal, ALU.mult
                                                    ).then_inc(stray_selected, 1)
                            dve.wait_ge(stray_selected, done + b + 1)
                            nc.vector.tensor_scalar(stray_rel[:, :], stray_rel[:, :], -float(P), None,
                                                    ALU.add).then_inc(stray_moved, 1)
                            dve.wait_ge(stray_summed, done + b + 1)
                            nc.vector.tensor_tensor(sums[l][:, ds(b * P, P)], sums[l][:, ds(b * P, P)],
                                                    win_ps[0][:, 0:P], ALU.add).then_inc(stray_added, 1)
                            dve.wait_ge(stray_added, done + b + 1)

            table_stage(0)
            edge_preparation()
            edge_stage(0)
            stray_stage(0)
            dve.sem_inc(layer_done[0], 1)
            table_stage(1)
            edge_stage(1)
            stray_stage(1)
            dve.sem_inc(layer_done[1], 1)

        @block.tensor
        def _(pe):
            pe.wait_ge(identity_ready, 2)
            pe.wait_ge(params_loaded, 96)

            def transpose(b, s):
                pe.wait_ge(h_rows_ready, b + 1)
                if past(b, 2):
                    pe.wait_ge(h_cols_ready[0], b - 1)
                nc.tensor.transpose(t_ps[s % 2][:, 0:P], h_rows[:, s, :], identity[:, :]).then_inc(transposed, 1)

            for l in range(2):
                if l == 0:
                    transpose(0, 0)

                def step(b, s, lap):
                    if l == 0 and exists(b + 1, BLOCKS):
                        transpose(b + 1, (s + 1) % SLOTS)
                    pe.wait_ge(h_cols_ready[l], b + 1)
                    if past(b, 2):
                        pe.wait_ge(y_staged[l], b - 1)
                        pe.wait_ge(root_added[l], b - 1)
                    nc.tensor.matmul(y_ps[s % 2][:, :], h_cols[:, s, :], W_sb[l][:, :], start=True, stop=True)
                    nc.tensor.matmul(r_ps[s % 2][:, 0:P], root_sb[l][:, :], h_cols[:, s, :], start=True, stop=True
                                     ).then_inc(y_multiplied[l], 1)
                over_blocks(pe, step)

                def reduce_group(g, s, lap):
                    if l == 0:
                        pe.wait_ge(select_ready, g + 1)
                    pe.wait_ge(rows_gathered[l][s], 16 * GROUP * (lap + 1))
                    if past(g, 2):
                        pe.wait_ge(window_added[l], g - 1)
                    for k in range(GROUP):
                        last = nc.tensor.matmul(win_ps[s % 2][:, 0:WINDOW], gathered[:, s, k, :],
                                                select[:, ds((g * GROUP + k) * WINDOW, WINDOW)],
                                                start=(k == 0), stop=(k == GROUP - 1))
                    last.then_inc(window_summed[l], 1)
                over_groups(pe, reduce_group)

                pe.wait_ge(flag_ready, 1)
                pe.wait_ge(window_added[l], GROUPS)
                strays = pe.value_load(stray_flag[0:1, 0:1], min_val=0, max_val=1)
                with pe.If(strays != 0):
                    with pe.Fori(0, TILES) as t:
                        done = (t + l * TILES) * BLOCKS
                        with pe.Fori(0, BLOCKS) as b:
                            pe.wait_ge(stray_gathered, (t + l * TILES + 1) * 16)
                            pe.wait_ge(stray_selected, done + b + 1)
                            nc.tensor.matmul(win_ps[0][:, 0:P], gathered[:, 0, 0, :], stray_select[:, :],
                                             start=True, stop=True).then_inc(stray_summed, 1)


def kernel(x, src, dst, edge_type_4, edge_weight, L0_gnn_W1, L0_gnn_root1, L0_gnn_b1,
           L0_gnn_W2, L0_gnn_root2, L0_gnn_b2):
    import numpy as np
    import concourse.bacc as bacc
    from concourse.bass_utils import run_bass_kernel_spmd

    def by_tile(a):
        return np.ascontiguousarray(np.pad(np.asarray(a), (0, TILES * P - N_EDGES), mode="edge").reshape(TILES, P).T)

    def relations_side_by_side(w):
        return np.ascontiguousarray(np.asarray(w).transpose(1, 0, 2).reshape(F, R * F))

    x_padded = np.pad(np.asarray(x), ((0, NODES - N_NODES), (0, 0)))
    dst_tiles = by_tile(dst)
    arrays = {
        "x_rows": x_padded,
        "x_cols": np.ascontiguousarray(x_padded.T),
        "src": by_tile(src),
        "dst": dst_tiles,
        "group_base": np.ascontiguousarray(dst_tiles[0, ::GROUP]),
        "edge_type": by_tile(edge_type_4),
        "edge_weight": by_tile(edge_weight),
        "W1": relations_side_by_side(L0_gnn_W1),
        "root1": np.asarray(L0_gnn_root1),
        "b1": np.asarray(L0_gnn_b1).reshape(F, 1),
        "W2": relations_side_by_side(L0_gnn_W2),
        "root2": np.asarray(L0_gnn_root2),
        "b2": np.asarray(L0_gnn_b2).reshape(F, 1),
    }
    nc = bacc.Bacc("TRN2", target_bir_lowering=False, num_devices=1)
    args = [nc.dram_tensor(name, a.shape, mybir.dt.from_np(a.dtype), kind="ExternalInput").ap()
            for name, a in arrays.items()]
    out = nc.dram_tensor("out_cols", (F, NODES), mybir.dt.float32, kind="ExternalOutput").ap()
    gnn_kernel(nc, *args, out)
    result = run_bass_kernel_spmd(nc, [arrays], core_ids=[0])
    return np.ascontiguousarray(result.results[0]["out_cols"].T[:N_NODES])
```

```python
import concourse.bass as bass
from concourse import mybir
from contextlib import ExitStack

P = 128
N_NODES = 3125
N_EDGES = 50000
F = 128
R = 4
BLOCKS = -(-N_NODES // P)
NODES = BLOCKS * P
GROUP = 4
TILES = -(-N_EDGES // (P * GROUP)) * GROUP
FULL_TILES = -(-N_EDGES // P)
GROUPS = TILES // GROUP
PAIR = 2
WINDOWS = TILES // PAIR
PER = GROUP // PAIR
NODES_IN_WINDOW = 24
COLS = NODES_IN_WINDOW * R
BCOLS = P * R
SLOTS = 4
LAPS = GROUPS // SLOTS
CHUNKS = 5
PER_CHUNK = BLOCKS // CHUNKS
BY_VECTOR = 2
MATMUL_SLOTS = (1, 3)
MATMUL_TILES = [(lap * SLOTS + s) * GROUP + GROUP - 1 for lap in range(1, LAPS) for s in MATMUL_SLOTS]
HALVES = (slice(0, 13), slice(13, BLOCKS))
PIECES = len(MATMUL_SLOTS) * len(HALVES)
PARTS = 3


def gnn_kernel(nc, x_rows, src, matmul_src, dst, window_base, edge_type, edge_weight,
               W1, root1, b1, W2, root2, b2, out_rows):
    fp32 = mybir.dt.float32
    bf16 = mybir.dt.bfloat16
    i16 = mybir.dt.int16
    i32 = mybir.dt.int32
    ALU = mybir.AluOpType
    ACT = mybir.ActivationFunctionType
    AX = mybir.AxisListType
    ds = bass.ds

    ctx = ExitStack()
    with ctx:
        def sb(name, shape, dt=fp32):
            return ctx.enter_context(nc.sbuf_tensor(name, shape, dt))

        def ps(name):
            return ctx.enter_context(nc.psum_tensor(name, [P, 512], fp32))

        def sem(name):
            return ctx.enter_context(nc.semaphore(name))

        rows = [nc.dram_tensor(f"rows{l}", [n, F], fp32, kind="Internal").ap() for l, n in enumerate((NODES, N_NODES))]
        x_sb = sb("x_sb", [P, BLOCKS * F])
        h_rows = [sb(f"h_rows{l}", [P, BLOCKS * F]) for l in range(2)]
        out_sb = h_rows[0]
        parts = [sb(f"parts{l}", [P, BLOCKS, PARTS, F], bf16) for l in range(2)]
        rest = sb("rest", [P, PER_CHUNK * F])
        sums = sb("sums", [P, NODES * R])
        W_sb = [sb(f"W_sb{l}", [P, R * F]) for l in range(2)]
        root_sb = [sb(f"root_sb{l}", [P, F]) for l in range(2)]
        b_sb = [sb(f"b_sb{l}", [1, F]) for l in range(2)]
        src_sb = sb("src_sb", [P, TILES], i32)
        type_sb = sb("type_sb", [P, TILES], i32)
        dst_sb = sb("dst_sb", [P, TILES], i32)
        base_sb = sb("base_sb", [P, WINDOWS], i32)
        first_col = sb("first_col", [P, WINDOWS], i32)
        ew_sb = sb("ew_sb", [P, TILES])
        weight = sb("weight", [P, TILES])
        minus_weight = sb("minus_weight", [P, TILES])
        column = sb("column", [P, TILES])
        key = sb("key", [P, TILES])
        inside = sb("inside", [P, TILES])
        regular = sb("regular", [P, TILES])
        finished_below = sb("finished_below", [P, TILES])
        tail_mask = sb("tail_mask", [P, TILES - N_EDGES // P])
        extremes = sb("extremes", [P, 2])
        extremes_all = sb("extremes_all", [P, 2])
        irregular = sb("irregular", [P, 1])
        irregular_all = sb("irregular_all", [P, 1])
        least_regular = sb("least_regular", [P, 1])
        irregular_flag = sb("irregular_flag", [P, 1], i32)
        ew_range = sb("ew_range", [P, 2])
        stats = sb("stats", [P, BLOCKS, 6])
        moments = sb("moments", [P, BLOCKS, 2])
        rstd = sb("rstd", [P, BLOCKS])
        shift = sb("shift", [P, BLOCKS])
        eps = sb("eps", [P, 1])
        numbers = sb("numbers", [P, BCOLS])
        node_id = sb("node_id", [P, BLOCKS])
        identity = sb("identity", [P, P])
        ones = sb("ones", [1, P])
        slot_index = sb("slot_index", [P, SLOTS, GROUP], i32)
        src_wide = sb("src_wide", [P, len(MATMUL_TILES) * P], i16)
        src_staging = [h_rows[1][:, :].bitcast(i32), parts[1][:, :, :, :].rearrange("p b q f -> p (b q f)").bitcast(i32)]
        node_table = sb("node_table", [P, BLOCKS, P], i16)
        source_onehot = sb("source_onehot", [P, BLOCKS, P], bf16)
        gathered = sb("gathered", [P, SLOTS, GROUP, F])
        select = sb("select", [P, SLOTS, GROUP, COLS])
        block_sums = sb("block_sums", [P, R, P])
        block_rows = sb("block_rows", [P, F])
        block_cols = sb("block_cols", [P, P])
        last_cols = sb("last_cols", [P, 2, P])
        edge_index = sb("edge_index", [P, 1], i32)
        edge_key = sb("edge_key", [P, 1])
        edge_select = sb("edge_select", [P, BCOLS])

        window_ps = [ps(f"window_ps{k}") for k in range(2)]
        block_ps = ps("block_ps")
        turned_ps = ps("turned_ps")
        other_block_ps = ps("other_block_ps")
        edge_ps = ps("edge_ps")
        gather_ps = [edge_ps, ps("gather_ps")]
        constants_ps = ps("constants_ps")
        window_numbers = constants_ps[:, 0:COLS]

        x_loaded = [sem(f"x_loaded{c}") for c in range(CHUNKS)]
        src_loaded = sem("src_loaded")
        edges_loaded = sem("edges_loaded")
        weights_loaded = sem("weights_loaded")
        params_loaded = sem("params_loaded")
        eps_ready = sem("eps_ready")
        constants_ready = sem("constants_ready")
        identity_ready = sem("identity_ready")
        sums_cleared = sem("sums_cleared")
        sums_wiped = sem("sums_wiped")
        last_sums_cleared = sem("last_sums_cleared")
        clears_begun = sem("clears_begun")
        parts_begun = sem("parts_begun")
        constants_placed = sem("constants_placed")
        first_parts = sem("first_parts")
        first_part_made = sem("first_part_made")
        last_turned = sem("last_turned")
        last_cols_taken = sem("last_cols_taken")
        parts_split = [sem(f"parts_split{l}") for l in range(2)]
        parts_again = sem("parts_again")
        src_widened = sem("src_widened")
        tables_ready = sem("tables_ready")
        onehot_ready = [sem(f"onehot_ready{l}") for l in range(2)]
        matmul_gathered = [sem(f"matmul_gathered{l}") for l in range(2)]
        matmul_rows_ready = [sem(f"matmul_rows_ready{l}") for l in range(2)]
        dve_step = sem("dve_step")
        stats_ready = sem("stats_ready")
        moments_ready = sem("moments_ready")
        std_ready = sem("std_ready")
        rstd_ready = sem("rstd_ready")
        norm_ready = sem("norm_ready")
        rows_by_act = sem("rows_by_act")
        rows_shifted = sem("rows_shifted")
        rows_by_pool = sem("rows_by_pool")
        rows_stored = sem("rows_stored")
        extremes_ready = sem("extremes_ready")
        extremes_reduced = sem("extremes_reduced")
        irregular_ready = sem("irregular_ready")
        irregular_reduced = sem("irregular_reduced")
        bases_ready = sem("bases_ready")
        flag_ready = sem("flag_ready")
        slot_indexed = [sem(f"slot_indexed{l}") for l in range(2)]
        gathers_begun = sem("gathers_begun")
        rows_gathered = [[sem(f"rows_gathered{l}_{s}") for s in range(SLOTS)] for l in range(2)]
        last_gathered = [[sem(f"last_gathered{l}_{k}") for k in range(GROUP)] for l in range(2)]
        key_distanced = [sem(f"key_distanced{l}") for l in range(2)]
        act_selects_begun = sem("act_selects_begun")
        select_by_act = [sem(f"select_by_act{l}") for l in range(2)]
        weights_ready = sem("weights_ready")
        select_ready = [sem(f"select_ready{l}") for l in range(2)]
        windows_summed = [sem(f"windows_summed{l}") for l in range(2)]
        window_added = [sem(f"window_added{l}") for l in range(2)]
        edge_indexed = sem("edge_indexed")
        edge_gathered = sem("edge_gathered")
        edge_moved = sem("edge_moved")
        edge_selected = sem("edge_selected")
        edge_summed = sem("edge_summed")
        edge_added = sem("edge_added")

        def finish_sems(tag):
            return {name: sem(f"{name}_{tag}") for name in
                    ("sums_taken", "sums_released", "rows_taken", "rows_turned", "cols_taken", "rooted", "multiplied", "staged", "stored")}

        regular_finish = [finish_sems(f"regular{l}") for l in range(2)]
        again_finish = [finish_sems(f"again{l}") for l in range(2)]

        block = ctx.enter_context(nc.Block())

        def if_irregular(eng):
            eng.wait_ge(flag_ready, 1)
            return eng.If(eng.value_load(irregular_flag[0:1, 0:1], min_val=0, max_val=1) != 0)

        LAST = BLOCKS - 1
        STAGED = len(MATMUL_TILES) * P // 2
        LAST_TILES = FULL_TILES - (GROUPS - 1) * GROUP
        TAIL = N_EDGES // P
        CLEAR_BY_POOL = NODES * R // 4
        CLEAR_BY_ACT = NODES * R * 5 // 8
        LAST_NODES = N_NODES - LAST * P
        BY_ACT = (3, 3, 3, 3, 4)

        def chunk_of(dram, c):
            return dram[c * PER_CHUNK * P:(c + 1) * PER_CHUNK * P, :].rearrange("(b p) f -> p b f", p=P)

        def is_static(n):
            return isinstance(n, int)

        def by_matmul(lap, s):
            return s in MATMUL_SLOTS and not (is_static(lap) and lap == 0)

        def piece_number(lap, q):
            return (lap - 1) * PIECES + q

        def matmul_number(lap, s):
            return (lap - 1) * len(MATMUL_SLOTS) + MATMUL_SLOTS.index(s)

        def chunk_cols(c):
            return slice(c * PER_CHUNK * F, (c + 1) * PER_CHUNK * F)

        @block.sync
        def _(sp):
            for c in range(CHUNKS):
                sp.dma_start(x_sb[:, chunk_cols(c)].rearrange("p (b f) -> p b f", f=F), chunk_of(x_rows, c)
                             ).then_inc(x_loaded[c], 16)
            sp.dma_start(dst_sb[:, :], dst).then_inc(edges_loaded, 16)
            sp.dma_start(base_sb[:, :], window_base.partition_broadcast(P)).then_inc(edges_loaded, 16)
            sp.dma_start(type_sb[:, :], edge_type).then_inc(edges_loaded, 16)
            sp.dma_start(src_sb[:, :], src).then_inc(src_loaded, 16)
            for c in range(CHUNKS):
                sp.wait_ge(rows_by_act, c + 1)
                sp.wait_ge(rows_by_pool, c + 1)
                sp.dma_start(chunk_of(rows[0], c), h_rows[0][:, chunk_cols(c)].rearrange("p (b f) -> p b f", f=F)
                             ).then_inc(rows_stored, 16)

            for k in range(2):
                sp.dma_start(src_staging[k][:, 0:STAGED], matmul_src[k * STAGED:(k + 1) * STAGED].partition_broadcast(P)
                             ).then_inc(src_widened, 16)

            def store(l, fin):
                made, goes = (h_rows[1], rows[1]) if l == 0 else (out_sb, out_rows)
                with sp.Fori(0, LAST) as b:
                    sp.wait_ge(fin["staged"], b + 1)
                    sp.dma_start(goes[ds(b * P, P), :], made[:, ds(b * F, F)]).then_inc(fin["stored"], 16)
                sp.wait_ge(fin["staged"], BLOCKS)
                sp.dma_start(goes[LAST * P:N_NODES, :], made[0:LAST_NODES, LAST * F:]).then_inc(fin["stored"], 16)
                sp.wait_ge(fin["stored"], 16 * BLOCKS)

            for l in range(2):
                store(l, regular_finish[l])
                with if_irregular(sp):
                    store(l, again_finish[l])

        @block.gpsimd
        def _(pool):
            nc.gpsimd.memset(eps[:, :], 1e-5).then_inc(eps_ready, 1)
            nc.gpsimd.iota(numbers[:, :], pattern=[[1, BCOLS]], base=0, channel_multiplier=0,
                           allow_small_or_imprecise_dtypes=True).then_inc(constants_ready, 1)
            first, last = 2 * GROUP, TILES - GROUP
            even = (last - first) // (SLOTS * GROUP)
            nc.gpsimd.memset(finished_below[:, 0:first], 0.0).then_inc(constants_ready, 1)
            nc.gpsimd.iota(finished_below[:, first:first + even * SLOTS * GROUP],
                           pattern=[[P, even], [0, SLOTS * GROUP]], base=0, channel_multiplier=0,
                           allow_small_or_imprecise_dtypes=True).then_inc(constants_ready, 1)
            nc.gpsimd.memset(finished_below[:, first + even * SLOTS * GROUP:last], float(even * P)
                             ).then_inc(constants_ready, 1)
            nc.gpsimd.memset(finished_below[:, last:], float(LAST * P)).then_inc(constants_ready, 1)
            nc.gpsimd.iota(node_id[:, :], pattern=[[P, BLOCKS]], base=0, channel_multiplier=1,
                           allow_small_or_imprecise_dtypes=True).then_inc(constants_ready, 1)
            nc.gpsimd.memset(ones[:, :], 1.0).then_inc(identity_ready, 1)
            nc.gpsimd.memset(identity[:, :], 0.0).then_inc(identity_ready, 1)
            nc.gpsimd.memset(tail_mask[:, :], 1.0).then_inc(identity_ready, 1)
            pool.wait_ge(identity_ready, 3)
            nc.gpsimd.affine_select(out=identity[:, :], in_=identity[:, :], compare_op=ALU.not_equal, fill=1.0,
                                    base=0, pattern=[[-1, P]], channel_multiplier=1).then_inc(identity_ready, 1)
            nc.gpsimd.affine_select(out=tail_mask[:, :], in_=tail_mask[:, :], compare_op=ALU.is_ge, fill=0.0,
                                    base=N_EDGES - 1 - TAIL * P, pattern=[[-P, TILES - TAIL]],
                                    channel_multiplier=-1).then_inc(constants_ready, 1)
            nc.gpsimd.memset(sums[:, 0:CLEAR_BY_POOL], 0.0).then_inc(sums_cleared, 1)
            for c in range(CHUNKS):
                pool.wait_ge(norm_ready, c + 1)
                mine = range(c * PER_CHUNK + BY_ACT[c], (c + 1) * PER_CHUNK)
                for b in mine:
                    shifted = nc.gpsimd.tensor_scalar(h_rows[0][:, b * F:(b + 1) * F], x_sb[:, b * F:(b + 1) * F],
                                                      rstd[:, b:b + 1], shift[:, b:b + 1], ALU.mult, ALU.add)
                shifted.then_inc(rows_shifted, 1)
                pool.wait_ge(rows_shifted, c + 1)
                share = h_rows[0][:, mine[0] * F:(mine[-1] + 1) * F]
                nc.gpsimd.tensor_scalar(share, share, 0.0, None, ALU.max).then_inc(rows_by_pool, 1)
            pool.wait_ge(extremes_ready, 1)
            nc.gpsimd.partition_all_reduce(extremes_all[:, :], extremes[:, :], P,
                                           bass.bass_isa.ReduceOp.max).then_inc(extremes_reduced, 1)

            def gather_tile(l, s, k, done):
                nc.gpsimd.indirect_dma_start(
                    out=gathered[:, s, k, :], out_offset=None, in_=rows[l],
                    in_offset=bass.IndirectOffsetOnAxis(ap=slot_index[:, s, k:k + 1], axis=0)).then_inc(done, 16)

            def gather(l, g, s, lap=0):
                pool.wait_ge(slot_indexed[l], g + 1)
                pool.sem_inc(gathers_begun, 1)
                for k in range(GROUP - by_matmul(lap, s)):
                    gather_tile(l, s, k, rows_gathered[l][s])

            for l in range(2):
                if l == 0:
                    pool.wait_ge(rows_stored, 16 * CHUNKS)
                else:
                    pool.wait_ge(regular_finish[0]["stored"], 16 * BLOCKS)
                    with if_irregular(pool):
                        pool.wait_ge(again_finish[0]["stored"], 16 * BLOCKS)
                for s in range(SLOTS):
                    gather(l, s, s)
                with pool.Fori(1, LAPS) as lap:
                    for s in range(SLOTS):
                        gather(l, lap * SLOTS + s, s, lap)
                if l == 0:
                    pool.wait_ge(irregular_ready, 1)
                    nc.gpsimd.partition_all_reduce(irregular_all[:, :], irregular[:, :], P,
                                                   bass.bass_isa.ReduceOp.max).then_inc(irregular_reduced, 1)
                gather(l, GROUPS - 2, 0)
                pool.wait_ge(slot_indexed[l], GROUPS)
                for k in range(LAST_TILES):
                    gather_tile(l, 1, k, last_gathered[l][k])
                with if_irregular(pool):
                    with pool.Fori(0, FULL_TILES) as t:
                        pool.wait_ge(edge_indexed, t + l * FULL_TILES + 1)
                        pool.sem_inc(gathers_begun, 1)
                        nc.gpsimd.indirect_dma_start(
                            out=gathered[:, 0, 0, :], out_offset=None, in_=rows[l],
                            in_offset=bass.IndirectOffsetOnAxis(ap=edge_index[:, :], axis=0),
                        ).then_inc(edge_gathered, 16)

        @block.scalar
        def _(act):
            act.dma_start(ew_sb[:, :], edge_weight).then_inc(weights_loaded, 16)
            act.wait_ge(eps_ready, 1)
            for c in range(CHUNKS):
                blocks = slice(c * PER_CHUNK, (c + 1) * PER_CHUNK)
                act.wait_ge(moments_ready, c + 1)
                nc.scalar.activation(rstd[:, blocks], moments[:, blocks, 1], ACT.Sqrt, bias=eps[:, :]
                                     ).then_inc(std_ready, 1)
                act.wait_ge(norm_ready, c + 1)
                for b in range(c * PER_CHUNK, c * PER_CHUNK + BY_ACT[c]):
                    last = nc.scalar.activation(h_rows[0][:, b * F:(b + 1) * F], x_sb[:, b * F:(b + 1) * F], ACT.Relu,
                                                bias=shift[:, b:b + 1], scale=rstd[:, b:b + 1])
                last.then_inc(rows_by_act, 1)

            def place_index(l, g, s):
                nc.scalar.copy(slot_index[:, s, :], src_sb[:, ds(g * GROUP, GROUP)]).then_inc(slot_indexed[l], 1)

            def build_select(l, g, s, tiles=range(BY_VECTOR, GROUP)):
                for k in tiles:
                    last = nc.scalar.activation(select[:, s, k, :], numbers[:, 0:COLS], ACT.Abs,
                                                bias=key[:, ds(g * GROUP + k, 1)], scale=-1.0)
                last.then_inc(key_distanced[l], 1)
                act.wait_ge(key_distanced[l], g + 1)
                act.sem_inc(act_selects_begun, 1)
                for k in tiles:
                    last = nc.scalar.activation(select[:, s, k, :], select[:, s, k, :], ACT.Relu,
                                                bias=weight[:, ds(g * GROUP + k, 1)],
                                                scale=minus_weight[:, ds(g * GROUP + k, 1)])
                last.then_inc(select_by_act[l], 1)

            def replace_index(l, g, s):
                act.wait_ge(windows_summed[l], g - SLOTS + 1)
                place_index(l, g, s)
                build_select(l, g, s, range(BY_VECTOR, LAST_TILES if is_static(g) and g == GROUPS - 1 else GROUP))

            def take_rows(l, fin, b):
                nc.scalar.copy(block_rows[:, :], h_rows[l][:, ds(b * F, F)]).then_inc(fin["rows_taken"], 1)

            def copy_sums(l, fin, b):
                nc.scalar.copy(block_sums[:, :, :], sums[:, ds(b * BCOLS, BCOLS)].rearrange("p (n r) -> p r n", r=R)
                               ).then_inc(fin["sums_taken"], 1)

            def take_sums(l, fin, b, added):
                act.wait_ge(*added)
                copy_sums(l, fin, b)
                act.wait_ge(fin["sums_taken"], b + 1)
                act.sem_inc(clears_begun, 1)
                if l == 0:
                    nc.scalar.memzero(sums[:, ds(b * BCOLS, BCOLS)]).then_inc(fin["sums_released"], 1)
                else:
                    act.sem_inc(fin["sums_released"], 1)

            def take_cols(l, fin, b):
                act.wait_ge(fin["rows_turned"], b + 1)
                nc.scalar.copy(block_cols[:, :], turned_ps[:, 0:P]).then_inc(fin["cols_taken"], 1)

            def new_block(l, fin, b, product=block_ps):
                act.wait_ge(fin["multiplied"], b + 1)
                if l == 0:
                    nc.scalar.activation(h_rows[1][:, ds(b * F, F)], product[:, 0:F], ACT.Relu
                                         ).then_inc(fin["staged"], 1)
                    act.wait_ge(fin["staged"], b + 1)
                    act.sem_inc(parts_begun, 1)
                    nc.scalar.copy(parts[1][:, ds(b, 1), 0, :], h_rows[1][:, None, ds(b * F, F)]
                                   ).then_inc(first_part_made, 1)

            act.wait_ge(src_loaded, 16)
            for s in range(SLOTS):
                place_index(0, s, s)
            nc.scalar.memzero(sums[:, CLEAR_BY_POOL:CLEAR_BY_ACT]).then_inc(sums_cleared, 1)
            act.wait_ge(weights_ready, 1)
            for s in range(SLOTS):
                build_select(0, s, s)
            act.wait_ge(rows_by_pool, CHUNKS)
            act.wait_ge(rows_by_act, CHUNKS)
            nc.scalar.copy(parts[0][:, :, 0, :], h_rows[0][:, :].rearrange("p (b f) -> p b f", f=F)
                           ).then_inc(first_parts, 1)
            act.wait_ge(constants_ready, 7)
            nc.scalar.copy(node_table[:, :, :], node_id[:, :, None].to_broadcast([P, BLOCKS, P])
                           ).then_inc(tables_ready, 1)
            act.wait_ge(src_widened, 32)
            for k in range(2):
                nc.scalar.copy(src_wide[:, k * STAGED:(k + 1) * STAGED], src_staging[k][:, 0:STAGED]
                               ).then_inc(tables_ready, 1)
            for l, (w, root, b) in enumerate(((W1, root1, b1), (W2, root2, b2))):
                act.dma_start(W_sb[l][:, :], w).then_inc(params_loaded, 16)
                act.dma_start(root_sb[l][:, :], root).then_inc(params_loaded, 16)
                act.dma_start(b_sb[l][:, :], b).then_inc(params_loaded, 16)
            for l in range(2):
                fin = regular_finish[l]
                for s in range(SLOTS):
                    replace_index(l, SLOTS + s, s)
                with act.Fori(2, LAPS) as lap:
                    b = lap - 2
                    replace_index(l, lap * SLOTS, 0)
                    take_rows(l, fin, b)
                    replace_index(l, lap * SLOTS + 1, 1)
                    take_cols(l, fin, b)
                    take_sums(l, fin, b, (window_added[l], ((lap - 1) * SLOTS + 2) * PER))
                    replace_index(l, lap * SLOTS + 2, 2)
                    new_block(l, fin, b)
                    replace_index(l, lap * SLOTS + 3, 3)
                replace_index(l, GROUPS - 2, 0)
                take_rows(l, fin, LAST - 2)
                replace_index(l, GROUPS - 1, 1)
                take_cols(l, fin, LAST - 2)
                take_sums(l, fin, LAST - 2, (window_added[l], ((LAPS - 1) * SLOTS + 2) * PER))
                act.wait_ge(last_turned, l + 1)
                nc.scalar.copy(last_cols[:, :, :], other_block_ps[:, P:3 * P].rearrange("p (k n) -> p k n", n=P)
                               ).then_inc(last_cols_taken, 1)
                new_block(l, fin, LAST - 2)
                act.wait_ge(window_added[l], (GROUPS - 1) * PER)
                copy_sums(l, fin, LAST - 1)
                if l == 0:
                    act.wait_ge(windows_summed[0], GROUPS)
                    for s in range(SLOTS):
                        place_index(1, s, s)
                        build_select(1, s, s)
                new_block(l, fin, LAST - 1, other_block_ps)
                new_block(l, fin, LAST, turned_ps)
                if l == 0:
                    act.wait_ge(window_added[0], WINDOWS)
                    nc.scalar.memzero(sums[:, (LAST - 1) * BCOLS:]).then_inc(last_sums_cleared, 1)
                with if_irregular(act):
                    fin = again_finish[l]
                    with act.Fori(0, BLOCKS) as b:
                        take_rows(l, fin, b)
                        take_cols(l, fin, b)
                        take_sums(l, fin, b, (edge_added, (l + 1) * FULL_TILES * BLOCKS))
                        new_block(l, fin, b)

        @block.vector
        def _(dve):
            steps = [0]

            def link(instruction):
                steps[0] += 1
                instruction.then_inc(dve_step, 1)
                dve.wait_ge(dve_step, steps[0])

            def chunk_moments(c):
                blocks = range(c * PER_CHUNK, (c + 1) * PER_CHUNK)
                dve.wait_ge(x_loaded[c], 16)
                for b in blocks:
                    last = nc.vector.bn_stats(stats[:, b, :], x_sb[:, b * F:(b + 1) * F])
                last.then_inc(stats_ready, 1)
                dve.wait_ge(stats_ready, c + 1)
                for b in blocks:
                    last = nc.vector.bn_aggr(moments[:, b, :], stats[:, b, :])
                last.then_inc(moments_ready, 1)

            def chunk_norm(c):
                blocks = slice(c * PER_CHUNK, (c + 1) * PER_CHUNK)
                dve.wait_ge(std_ready, c + 1)
                nc.vector.reciprocal(rstd[:, blocks], rstd[:, blocks]).then_inc(rstd_ready, 1)
                dve.wait_ge(rstd_ready, c + 1)
                nc.vector.scalar_tensor_tensor(out=shift[:, blocks], in0=moments[:, blocks, 0], scalar=-1.0,
                                               in1=rstd[:, blocks], op0=ALU.mult, op1=ALU.mult
                                               ).then_inc(norm_ready, 1)

            def by_window(a):
                return a[:, :].rearrange("p (w k) -> p w k", k=PAIR)

            def edge_weights():
                dve.wait_ge(extremes_reduced, 1)
                link(nc.vector.tensor_scalar(ew_range[:, 0:1], extremes_all[:, 0:1], extremes_all[:, 1:2], 1e-8,
                                             ALU.add, ALU.add))
                link(nc.vector.reciprocal(ew_range[:, 1:2], ew_range[:, 0:1]))
                link(nc.vector.tensor_scalar(weight[:, :], ew_sb[:, :], extremes_all[:, 1:2], ew_range[:, 1:2],
                                             ALU.add, ALU.mult))
                dve.wait_ge(constants_ready, 7)
                link(nc.vector.tensor_tensor(weight[:, TAIL:], weight[:, TAIL:], tail_mask[:, :], ALU.mult))
                nc.vector.tensor_scalar(minus_weight[:, :], weight[:, :], -1.0, None, ALU.mult
                                        ).then_inc(weights_ready, 1)

            def edge_keys():
                dve.wait_ge(edges_loaded, 48)
                link(nc.vector.tensor_scalar(first_col[:, :], base_sb[:, :], float(R), None, ALU.mult))
                link(nc.vector.scalar_tensor_tensor(out=column[:, :], in0=dst_sb[:, :], scalar=float(R),
                                                    in1=type_sb[:, :], op0=ALU.mult, op1=ALU.add))
                link(nc.vector.tensor_tensor(by_window(key), by_window(column),
                                             first_col[:, :, None].to_broadcast([P, WINDOWS, PAIR]), ALU.subtract))

            def edge_regularity():
                link(nc.vector.tensor_scalar(inside[:, :], key[:, :], 0.0, None, ALU.is_ge))
                link(nc.vector.scalar_tensor_tensor(out=inside[:, :], in0=key[:, :], scalar=float(COLS),
                                                    in1=inside[:, :], op0=ALU.is_lt, op1=ALU.mult))
                link(nc.vector.tensor_tensor(regular[:, :], dst_sb[:, :], finished_below[:, :], ALU.is_ge))
                link(nc.vector.tensor_tensor(regular[:, :], regular[:, :], inside[:, :], ALU.mult))
                link(nc.vector.tensor_reduce(out=least_regular[:, :], in_=regular[:, :], axis=AX.X, op=ALU.min))
                nc.vector.tensor_scalar(irregular[:, :], least_regular[:, :], -1.0, 1.0, ALU.mult, ALU.add
                                        ).then_inc(irregular_ready, 1)

            def build_select(l, g, s, tiles=BY_VECTOR):
                for k in range(tiles):
                    t = g * GROUP + k
                    last = nc.vector.tensor_scalar(select[:, s, k, :], window_numbers,
                                                   key[:, ds(t, 1)], weight[:, ds(t, 1)], ALU.is_equal, ALU.mult)
                last.then_inc(select_ready[l], 1)

            def add_windows(l, g, s):
                cols = [dve.value_load(first_col[0:1, ds(g * PER + j, 1)], min_val=0, max_val=(N_NODES - 1) * R)
                        for j in range(PER)]
                dve.wait_ge(windows_summed[l], g + 1)
                for j in range(PER):
                    if not is_static(g) or g * PER + j > 0:
                        dve.wait_ge(window_added[l], g * PER + j)
                    nc.vector.tensor_tensor(sums[:, ds(cols[j], COLS)], sums[:, ds(cols[j], COLS)],
                                            window_ps[s % 2][:, j * COLS:(j + 1) * COLS],
                                            ALU.add).then_inc(window_added[l], 1)

            def sums_released(l, fin, b):
                dve.wait_ge(fin["sums_released"], b + 1)

            def build_piece(l, lap, q):
                before = piece_number(lap, q) - len(HALVES)
                if not is_static(before) or before >= 0:
                    dve.wait_ge(matmul_gathered[l], before + 1)
                k, blocks = q // len(HALVES), HALVES[q % len(HALVES)]
                tile = matmul_number(lap, MATMUL_SLOTS[k])
                nc.vector.tensor_tensor(source_onehot[:, blocks, :],
                                        src_wide[:, None, ds(tile * P, P)
                                                 ].to_broadcast([P, blocks.stop - blocks.start, P]),
                                        node_table[:, blocks, :], ALU.is_equal).then_inc(onehot_ready[l], 1)

            def join_parts(l, lap, s):
                dve.wait_ge(matmul_gathered[l], (matmul_number(lap, s) + 1) * len(HALVES))
                dve.wait_ge(windows_summed[l], (lap - 1) * SLOTS + s + 1)
                nc.vector.tensor_reduce(out=gathered[:, s, GROUP - 1, :],
                                        in_=gather_ps[MATMUL_SLOTS.index(s)][:, 0:PARTS * F].rearrange("p (q f) -> p f q", f=F),
                                        axis=AX.X, op=ALU.add).then_inc(matmul_rows_ready[l], 1)

            def split_rows(l, b, count, done):
                h = h_rows[l][:, ds(b * F, count * F)].rearrange("p (b f) -> p b f", f=F)
                left = rest[:, 0:count * F].rearrange("p (b f) -> p b f", f=F)
                part = [parts[l][:, ds(b, count), q, :] for q in range(PARTS)]
                nc.vector.tensor_tensor(left, h, part[0], ALU.subtract)
                nc.vector.tensor_tensor(part[1], h, part[0], ALU.subtract).then_inc(done, 1)
                return left, part

            def split_rest(left, part, done):
                nc.vector.tensor_tensor(part[2], left, part[1], ALU.subtract).then_inc(done, 1)

            def result_block(l, fin, b, product=block_ps):
                dve.wait_ge(fin["multiplied"], b + 1)
                if l == 1:
                    nc.vector.tensor_tensor(out_sb[:, ds(b * F, F)], product[:, 0:F], x_sb[:, ds(b * F, F)], ALU.add
                                            ).then_inc(fin["staged"], 1)

            def split(l, b, count, done, n):
                left, part = split_rows(l, b, count, done)
                dve.wait_ge(done, n + 1)
                split_rest(left, part, done)
                dve.wait_ge(done, n + 2)

            def every_edge(l):
                nc.vector.memset(sums[:, :], 0.0).then_inc(sums_wiped, 1)
                dve.wait_ge(sums_wiped, l + 1)
                with dve.Fori(0, FULL_TILES) as t:
                    done = (t + l * FULL_TILES) * BLOCKS
                    nc.vector.tensor_copy(edge_index[:, :], src_sb[:, ds(t, 1)]).then_inc(edge_indexed, 1)
                    nc.vector.tensor_copy(edge_key[:, :], column[:, ds(t, 1)]).then_inc(edge_moved, 1)
                    with dve.Fori(0, BLOCKS) as b:
                        dve.wait_ge(edge_moved, done + t + l * FULL_TILES + b + 1)
                        nc.vector.tensor_scalar(edge_select[:, :], numbers[:, :], edge_key[:, :],
                                                weight[:, ds(t, 1)], ALU.is_equal, ALU.mult
                                                ).then_inc(edge_selected, 1)
                        dve.wait_ge(edge_selected, done + b + 1)
                        nc.vector.tensor_scalar(edge_key[:, :], edge_key[:, :], -float(BCOLS), None,
                                                ALU.add).then_inc(edge_moved, 1)
                        dve.wait_ge(edge_summed, done + b + 1)
                        nc.vector.tensor_tensor(sums[:, ds(b * BCOLS, BCOLS)], sums[:, ds(b * BCOLS, BCOLS)],
                                                edge_ps[:, :], ALU.add).then_inc(edge_added, 1)
                        dve.wait_ge(edge_added, done + b + 1)

            for c in range(CHUNKS):
                chunk_moments(c)
                if c:
                    chunk_norm(c - 1)
            chunk_norm(CHUNKS - 1)
            dve.wait_ge(weights_loaded, 16)
            nc.vector.tensor_reduce(out=extremes[:, 0:1], in_=ew_sb[:, :], axis=AX.X, op=ALU.max)
            nc.vector.tensor_reduce(out=extremes[:, 1:2], in_=ew_sb[:, :], axis=AX.X, op=ALU.min, negate=True
                                    ).then_inc(extremes_ready, 1)
            edge_keys()
            edge_weights()
            nc.vector.tensor_copy(window_numbers, numbers[:, 0:COLS]).then_inc(constants_placed, 1)
            dve.wait_ge(constants_placed, 1)

            for l in range(2):
                fin = regular_finish[l]
                for g in range(SLOTS):
                    build_select(l, g, g)
                if l == 0:
                    nc.vector.memset(sums[:, CLEAR_BY_ACT:], 0.0).then_inc(sums_cleared, 1)
                    dve.wait_ge(sums_cleared, 3)
                else:
                    dve.wait_ge(regular_finish[0]["sums_released"], LAST - 1)
                    dve.wait_ge(last_sums_cleared, 1)

                def lap_of_groups(lap):
                    b = lap - 1
                    started = not is_static(lap) or lap > 0
                    for s in range(SLOTS):
                        g = lap * SLOTS + s
                        if s + 1 in MATMUL_SLOTS and started:
                            join_parts(l, lap, s + 1)
                        add_windows(l, g, s)
                        if l == 0 and is_static(lap) and lap == 0:
                            dve.wait_ge(first_parts, 1)
                            for c in (s, s + 1) if s == SLOTS - 1 else (s,):
                                split(0, c * PER_CHUNK, PER_CHUNK, parts_split[0], 2 * c)
                        if l == 1 and is_static(lap) and lap == 0 and s == 0:
                            dve.wait_ge(first_part_made, BLOCKS)
                            split(1, LAST - 2, 3, parts_split[1], 2 * (BLOCKS - 3))
                        if s == 0 and started:
                            build_piece(l, lap, 3)
                        if s > 0 and not (is_static(lap) and lap == LAPS - 1):
                            if l == 0 and is_static(lap) and lap == 0 and s == 1:
                                dve.wait_ge(tables_ready, 3)
                            build_piece(l, lap + 1, s - 1)
                        if not is_static(g) or g + SLOTS < GROUPS:
                            build_select(l, g + SLOTS, s)
                        if l == 0 and is_static(lap) and lap == 1 and s == 0:
                            edge_regularity()
                        if s == 1 and started:
                            sums_released(l, fin, b)
                        if s == 3 and started:
                            result_block(l, fin, b)
                            if l == 0 and not (is_static(lap) and lap == LAPS - 1):
                                dve.wait_ge(first_part_made, b + 1)
                                split(1, b, 1, parts_split[1], 2 * b)

                lap_of_groups(0)
                lap_of_groups(1)
                with dve.Fori(2, LAPS - 1) as lap:
                    lap_of_groups(lap)
                lap_of_groups(LAPS - 1)
                if l == 0:
                    dve.wait_ge(irregular_reduced, 1)
                    nc.vector.tensor_copy(irregular_flag[:, :], irregular_all[:, :]).then_inc(flag_ready, 1)
                add_windows(l, GROUPS - 2, 0)
                dve.wait_ge(fin["sums_taken"], LAST)
                add_windows(l, GROUPS - 1, 1)
                result_block(l, fin, LAST - 1, other_block_ps)
                result_block(l, fin, LAST, turned_ps)
                with if_irregular(dve):
                    dve.wait_ge(fin["stored"], 16 * BLOCKS)
                    if l == 0:
                        dve.wait_ge(last_sums_cleared, 1)
                    every_edge(l)
                    fin = again_finish[l]
                    with dve.Fori(0, BLOCKS) as b:
                        result_block(l, fin, b)
                        if l == 0:
                            dve.wait_ge(first_part_made, BLOCKS + b + 1)
                            split(1, b, 1, parts_again, 2 * b)
                    if l == 0:
                        dve.wait_ge(fin["sums_released"], BLOCKS)

        @block.tensor
        def _(pe):
            pe.wait_ge(identity_ready, 4)

            def sum_window(s, k, last_tile):
                j = k // PAIR
                return nc.tensor.matmul(window_ps[s % 2][:, j * COLS:(j + 1) * COLS], gathered[:, s, k, :],
                                        select[:, s, k, :], start=(k % PAIR == 0),
                                        stop=(k % PAIR == PAIR - 1 or k == last_tile))

            def selects_built(l, g):
                pe.wait_ge(select_ready[l], g + 1)
                pe.wait_ge(select_by_act[l], g + 1)
                if not is_static(g) or g >= 2:
                    pe.wait_ge(window_added[l], (g - 1) * PER)

            def sum_group(l, g, s, turn):
                selects_built(l, g)
                if s in MATMUL_SLOTS:
                    pe.wait_ge(rows_gathered[l][s], 16 * ((GROUP - 1) * (turn + 1) + 1))
                else:
                    pe.wait_ge(rows_gathered[l][s], 16 * GROUP * (turn + 1))
                if by_matmul(turn, s):
                    pe.wait_ge(matmul_rows_ready[l], matmul_number(turn, s) + 1)
                for k in range(GROUP):
                    last = sum_window(s, k, GROUP - 1)
                last.then_inc(windows_summed[l], 1)

            def gather_piece(l, lap, q):
                pe.wait_ge(onehot_ready[l], piece_number(lap, q) + 1)
                for b in range(BLOCKS)[HALVES[q % len(HALVES)]]:
                    last = nc.tensor.matmul(gather_ps[q // len(HALVES)][:, 0:PARTS * F], source_onehot[:, b, :],
                                            parts[l][:, b, :, :].rearrange("p q f -> p (q f)"),
                                            start=(b == 0), stop=(b == BLOCKS - 1))
                last.then_inc(matmul_gathered[l], 1)

            def sum_last_window(l):
                selects_built(l, GROUPS - 1)
                for k in range(LAST_TILES):
                    pe.wait_ge(last_gathered[l][k], 16)
                    last = sum_window(1, k, LAST_TILES - 1)
                last.then_inc(windows_summed[l], 1)

            def turn_rows(l, fin, b):
                pe.wait_ge(fin["rows_taken"], b + 1)
                nc.tensor.transpose(turned_ps[:, 0:P], block_rows[:, :], identity[:, :]
                                    ).then_inc(fin["rows_turned"], 1)

            def bias_and_root(l, fin, b, product=block_ps):
                nc.tensor.matmul(product[:, 0:F], ones[:, :], b_sb[l][:, :], start=True, stop=False)
                pe.wait_ge(fin["cols_taken"], b + 1)
                nc.tensor.matmul(product[:, 0:F], block_cols[:, :], root_sb[l][:, :], start=False, stop=False
                                 ).then_inc(fin["rooted"], 1)

            def turn_last_rows(l):
                for k in range(2):
                    last = nc.tensor.transpose(other_block_ps[:, (k + 1) * P:(k + 2) * P],
                                               h_rows[l][:, (LAST - 1 + k) * F:(LAST + k) * F], identity[:, :])
                last.then_inc(last_turned, 1)

            def last_bias_and_root(l):
                pe.wait_ge(last_cols_taken, l + 1)
                for k, product in enumerate((other_block_ps, turned_ps)):
                    nc.tensor.matmul(product[:, 0:F], ones[:, :], b_sb[l][:, :], start=True, stop=False)
                    nc.tensor.matmul(product[:, 0:F], last_cols[:, k, :], root_sb[l][:, :], start=False, stop=False)

            def relations(l, fin, b, product=block_ps, block_sums=block_sums):
                for r in range(R):
                    last = nc.tensor.matmul(product[:, 0:F], block_sums[:, r, :], W_sb[l][:, r * F:(r + 1) * F],
                                            start=False, stop=(r == R - 1))
                last.then_inc(fin["multiplied"], 1)

            def multiply_block(l, fin, b):
                bias_and_root(l, fin, b)
                pe.wait_ge(fin["sums_taken"], b + 1)
                relations(l, fin, b)

            def staged(l, fin, b):
                pe.wait_ge(fin["staged"], b + 1)

            for l in range(2):
                fin = regular_finish[l]
                for s in range(SLOTS):
                    sum_group(l, s, s, 0)
                pe.wait_ge(params_loaded, 96)
                pe.wait_ge(parts_split[l], 2 * (CHUNKS if l == 0 else BLOCKS - 2))
                if l == 1:
                    with if_irregular(pe):
                        pe.wait_ge(parts_again, 2 * BLOCKS)

                gather_piece(l, 1, 0)
                gather_piece(l, 1, 1)

                def lap_of_groups(lap):
                    b = lap - 1
                    sum_group(l, lap * SLOTS, 0, lap)
                    gather_piece(l, lap, 2)
                    turn_rows(l, fin, b)
                    if is_static(lap) and lap == LAPS - 1:
                        turn_last_rows(l)
                    sum_group(l, lap * SLOTS + 1, 1, lap)
                    gather_piece(l, lap, 3)
                    sum_group(l, lap * SLOTS + 2, 2, lap)
                    if not (is_static(lap) and lap == LAPS - 1):
                        gather_piece(l, lap + 1, 0)
                    multiply_block(l, fin, b)
                    if is_static(lap) and lap == LAPS - 1:
                        last_bias_and_root(l)
                    sum_group(l, lap * SLOTS + 3, 3, lap)
                    if not (is_static(lap) and lap == LAPS - 1):
                        gather_piece(l, lap + 1, 1)
                    staged(l, fin, b)

                with pe.Fori(1, LAPS - 1) as lap:
                    lap_of_groups(lap)
                lap_of_groups(LAPS - 1)
                sum_group(l, GROUPS - 2, 0, LAPS)
                sum_last_window(l)
                pe.wait_ge(fin["sums_taken"], LAST)
                relations(l, fin, LAST - 1, other_block_ps)
                pe.wait_ge(window_added[l], WINDOWS)
                relations(l, fin, LAST, turned_ps,
                          sums[:, LAST * BCOLS:].rearrange("p (n r) -> p r n", r=R))
                with if_irregular(pe):
                    staged(l, fin, BLOCKS - 1)
                    with pe.Fori(0, FULL_TILES) as t:
                        done = (t + l * FULL_TILES) * BLOCKS
                        with pe.Fori(0, BLOCKS) as b:
                            pe.wait_ge(edge_gathered, (t + l * FULL_TILES + 1) * 16)
                            pe.wait_ge(edge_selected, done + b + 1)
                            nc.tensor.matmul(edge_ps[:, :], gathered[:, 0, 0, :], edge_select[:, :],
                                             start=True, stop=True).then_inc(edge_summed, 1)
                    fin = again_finish[l]
                    with pe.Fori(0, BLOCKS) as b:
                        turn_rows(l, fin, b)
                        multiply_block(l, fin, b)
                        staged(l, fin, b)


def kernel(x, src, dst, edge_type_4, edge_weight, L0_gnn_W1, L0_gnn_root1, L0_gnn_b1,
           L0_gnn_W2, L0_gnn_root2, L0_gnn_b2):
    import numpy as np
    import concourse.bacc as bacc
    from concourse.bass_utils import run_bass_kernel_spmd

    def by_tile(a):
        return np.ascontiguousarray(np.pad(np.asarray(a), (0, TILES * P - N_EDGES), mode="edge").reshape(TILES, P).T)

    def relations_side_by_side(w):
        return np.ascontiguousarray(np.asarray(w).transpose(1, 0, 2).reshape(F, R * F))

    x_padded = np.pad(np.asarray(x), ((0, NODES - N_NODES), (0, 0)))
    dst_tiles = by_tile(dst)
    arrays = {
        "x_rows": x_padded,
        "src": by_tile(src),
        "matmul_src": np.ascontiguousarray(by_tile(src)[:, MATMUL_TILES].T).reshape(-1),
        "dst": dst_tiles,
        "window_base": np.ascontiguousarray(dst_tiles[0, ::PAIR]),
        "edge_type": by_tile(edge_type_4),
        "edge_weight": by_tile(edge_weight),
        "W1": relations_side_by_side(L0_gnn_W1),
        "root1": np.asarray(L0_gnn_root1),
        "b1": np.asarray(L0_gnn_b1).reshape(1, F),
        "W2": relations_side_by_side(L0_gnn_W2),
        "root2": np.asarray(L0_gnn_root2),
        "b2": np.asarray(L0_gnn_b2).reshape(1, F),
    }
    nc = bacc.Bacc("TRN2", target_bir_lowering=False, num_devices=1)
    args = [nc.dram_tensor(name, a.shape, mybir.dt.from_np(a.dtype), kind="ExternalInput").ap()
            for name, a in arrays.items()]
    out = nc.dram_tensor("out_rows", (N_NODES, F), mybir.dt.float32, kind="ExternalOutput").ap()
    gnn_kernel(nc, *args, out)
    result = run_bass_kernel_spmd(nc, [arrays], core_ids=[0])
    return result.results[0]["out_rows"]
```

```python
import concourse.bass as bass
from concourse import mybir
from contextlib import ExitStack

P = 128
N_NODES = 3125
N_EDGES = 50000
F = 128
R = 4
BLOCKS = -(-N_NODES // P)
NODES = BLOCKS * P
GROUP = 4
TILES = -(-N_EDGES // (P * GROUP)) * GROUP
FULL_TILES = -(-N_EDGES // P)
GROUPS = TILES // GROUP
PAIR = 2
WINDOWS = TILES // PAIR
PER = GROUP // PAIR
NODES_IN_WINDOW = 24
COLS = NODES_IN_WINDOW * R
BCOLS = P * R
SLOTS = 4
LAPS = GROUPS // SLOTS
CHUNKS = 5
PER_CHUNK = BLOCKS // CHUNKS
BY_VECTOR = 2
MATMUL_SLOTS = (1, 3)
MATMUL_FROM = (2, 0)
MATMUL_TILES = [(lap * SLOTS + s) * GROUP + GROUP - 1 for lap in range(LAPS) for s in MATMUL_SLOTS]
HALVES = (slice(0, 13), slice(13, BLOCKS))
PIECES = len(MATMUL_SLOTS) * len(HALVES)
PARTS = 3


def gnn_kernel(nc, x_rows, src, matmul_src, dst, window_base, edge_type, edge_weight,
               W1, root1, b1, W2, root2, b2, out_rows):
    fp32 = mybir.dt.float32
    bf16 = mybir.dt.bfloat16
    i16 = mybir.dt.int16
    i32 = mybir.dt.int32
    ALU = mybir.AluOpType
    ACT = mybir.ActivationFunctionType
    AX = mybir.AxisListType
    ds = bass.ds

    ctx = ExitStack()
    with ctx:
        def sb(name, shape, dt=fp32):
            return ctx.enter_context(nc.sbuf_tensor(name, shape, dt))

        def ps(name):
            return ctx.enter_context(nc.psum_tensor(name, [P, 512], fp32))

        def sem(name):
            return ctx.enter_context(nc.semaphore(name))

        rows = [nc.dram_tensor(f"rows{l}", [n, F], fp32, kind="Internal").ap() for l, n in enumerate((NODES, N_NODES))]
        x_sb = sb("x_sb", [P, BLOCKS * F])
        h_rows = [sb(f"h_rows{l}", [P, BLOCKS * F]) for l in range(2)]
        out_sb = h_rows[0]
        parts = [sb(f"parts{l}", [P, BLOCKS, PARTS, F], bf16) for l in range(2)]
        rest = sb("rest", [P, PER_CHUNK * F])
        sums = sb("sums", [P, NODES * R])
        W_sb = [sb(f"W_sb{l}", [P, R * F]) for l in range(2)]
        root_sb = [sb(f"root_sb{l}", [P, F]) for l in range(2)]
        b_sb = [sb(f"b_sb{l}", [1, F]) for l in range(2)]
        src_sb = sb("src_sb", [P, TILES], i32)
        type_sb = sb("type_sb", [P, TILES], i32)
        dst_sb = sb("dst_sb", [P, TILES], i32)
        base_sb = sb("base_sb", [P, WINDOWS], i32)
        first_nodes = sb("first_nodes", [P, GROUPS], i32)
        first_col = sb("first_col", [P, WINDOWS], i32)
        ew_sb = sb("ew_sb", [P, TILES])
        weight = sb("weight", [P, TILES])
        minus_weight = sb("minus_weight", [P, TILES])
        column = sb("column", [P, TILES])
        key = sb("key", [P, TILES])
        inside = sb("inside", [P, TILES])
        regular = sb("regular", [P, TILES])
        finished_below = sb("finished_below", [P, TILES])
        tail_mask = sb("tail_mask", [P, TILES - N_EDGES // P])
        extremes = sb("extremes", [P, 2])
        extremes_all = sb("extremes_all", [P, 2])
        irregular = sb("irregular", [P, 1])
        irregular_all = sb("irregular_all", [P, 1])
        least_regular = sb("least_regular", [P, 1])
        irregular_flag = sb("irregular_flag", [P, 1], i32)
        ew_range = sb("ew_range", [P, 2])
        stats = sb("stats", [P, BLOCKS, 6])
        moments = sb("moments", [P, BLOCKS, 2])
        rstd = sb("rstd", [P, BLOCKS])
        shift = sb("shift", [P, BLOCKS])
        eps = sb("eps", [P, 1])
        numbers = sb("numbers", [P, BCOLS])
        node_id = sb("node_id", [P, BLOCKS])
        identity = sb("identity", [P, P])
        ones = sb("ones", [1, P])
        slot_index = sb("slot_index", [P, SLOTS, GROUP], i32)
        src_wide = sb("src_wide", [P, len(MATMUL_TILES) * P], i16)
        src_staging = [h_rows[1][:, :].bitcast(i32),
                       parts[1][:, :, :, :].rearrange("p b q f -> p (b q f)").bitcast(i32)]
        node_table = sb("node_table", [P, BLOCKS, P], i16)
        source_onehot = sb("source_onehot", [P, BLOCKS, P], bf16)
        gathered = sb("gathered", [P, SLOTS, GROUP, F])
        select = sb("select", [P, SLOTS, GROUP, COLS])
        block_sums = sb("block_sums", [P, R, P])
        block_rows = sb("block_rows", [P, F])
        block_cols = sb("block_cols", [P, P])
        last_cols = sb("last_cols", [P, 2, P])
        edge_index = sb("edge_index", [P, 1], i32)
        edge_key = sb("edge_key", [P, 1])
        edge_select = sb("edge_select", [P, BCOLS])

        window_ps = [ps(f"window_ps{k}") for k in range(2)]
        block_ps = ps("block_ps")
        turned_ps = ps("turned_ps")
        other_block_ps = ps("other_block_ps")
        edge_ps = ps("edge_ps")
        gather_ps = [edge_ps, ps("gather_ps")]
        constants_ps = ps("constants_ps")
        window_numbers = constants_ps[:, 0:COLS]

        x_loaded = [sem(f"x_loaded{c}") for c in range(CHUNKS)]
        src_loaded = sem("src_loaded")
        edges_loaded = sem("edges_loaded")
        weights_loaded = sem("weights_loaded")
        params_loaded = sem("params_loaded")
        eps_ready = sem("eps_ready")
        constants_ready = sem("constants_ready")
        identity_ready = sem("identity_ready")
        sums_cleared = sem("sums_cleared")
        sums_wiped = sem("sums_wiped")
        last_sums_cleared = sem("last_sums_cleared")
        clears_begun = sem("clears_begun")
        parts_begun = sem("parts_begun")
        constants_placed = sem("constants_placed")
        first_parts = sem("first_parts")
        first_part_made = sem("first_part_made")
        last_turned = sem("last_turned")
        last_cols_taken = sem("last_cols_taken")
        parts_split = [sem(f"parts_split{l}") for l in range(2)]
        parts_again = sem("parts_again")
        src_widened = sem("src_widened")
        tables_ready = sem("tables_ready")
        onehot_ready = [sem(f"onehot_ready{l}") for l in range(2)]
        matmul_gathered = [sem(f"matmul_gathered{l}") for l in range(2)]
        matmul_rows_ready = [sem(f"matmul_rows_ready{l}") for l in range(2)]
        dve_step = sem("dve_step")
        stats_ready = sem("stats_ready")
        moments_ready = sem("moments_ready")
        std_ready = sem("std_ready")
        rstd_ready = sem("rstd_ready")
        norm_ready = sem("norm_ready")
        rows_by_act = sem("rows_by_act")
        rows_shifted = sem("rows_shifted")
        rows_by_pool = sem("rows_by_pool")
        rows_stored = sem("rows_stored")
        extremes_ready = sem("extremes_ready")
        extremes_reduced = sem("extremes_reduced")
        irregular_ready = sem("irregular_ready")
        irregular_reduced = sem("irregular_reduced")
        flag_ready = sem("flag_ready")
        slot_indexed = [sem(f"slot_indexed{l}") for l in range(2)]
        gathers_begun = sem("gathers_begun")
        rows_gathered = [[sem(f"rows_gathered{l}_{s}") for s in range(SLOTS)] for l in range(2)]
        last_gathered = [[sem(f"last_gathered{l}_{k}") for k in range(GROUP)] for l in range(2)]
        key_distanced = [sem(f"key_distanced{l}") for l in range(2)]
        act_selects_begun = sem("act_selects_begun")
        select_by_act = [sem(f"select_by_act{l}") for l in range(2)]
        weights_ready = sem("weights_ready")
        select_ready = [sem(f"select_ready{l}") for l in range(2)]
        windows_summed = [sem(f"windows_summed{l}") for l in range(2)]
        window_added = [sem(f"window_added{l}") for l in range(2)]
        edge_indexed = sem("edge_indexed")
        edge_gathered = sem("edge_gathered")
        edge_moved = sem("edge_moved")
        edge_selected = sem("edge_selected")
        edge_summed = sem("edge_summed")
        edge_added = sem("edge_added")

        def finish_sems(tag):
            return {name: sem(f"{name}_{tag}") for name in
                    ("sums_taken", "sums_released", "rows_taken", "rows_turned", "cols_taken", "rooted", "multiplied",
                     "staged", "stored")}

        regular_finish = [finish_sems(f"regular{l}") for l in range(2)]
        again_finish = [finish_sems(f"again{l}") for l in range(2)]

        block = ctx.enter_context(nc.Block())

        def if_irregular(eng):
            eng.wait_ge(flag_ready, 1)
            return eng.If(eng.value_load(irregular_flag[0:1, 0:1], min_val=0, max_val=1) != 0)

        LAST = BLOCKS - 1
        SPLIT_LATER = LAPS - 3
        STAGED_PIECES = 4
        NODE_UNIT = N_NODES
        assert NODE_UNIT * N_NODES <= 1 << 24 and PER == 2
        STAGED = len(MATMUL_TILES) * P // 2
        LAST_TILES = FULL_TILES - (GROUPS - 1) * GROUP
        TAIL = N_EDGES // P
        CLEAR_BY_POOL = NODES * R // 4
        CLEAR_BY_ACT = NODES * R * 5 // 8
        LAST_NODES = N_NODES - LAST * P
        BY_ACT = (3, 3, 3, 3, 4)

        def chunk_of(dram, c):
            return dram[c * PER_CHUNK * P:(c + 1) * PER_CHUNK * P, :].rearrange("(b p) f -> p b f", p=P)

        def is_static(n):
            return isinstance(n, int)

        def matmul_lap(l, lap):
            return not is_static(lap) or MATMUL_FROM[l] <= lap < LAPS

        def by_matmul(l, lap, s):
            return s in MATMUL_SLOTS and matmul_lap(l, lap)

        def piece_number(l, lap, q):
            return (lap - MATMUL_FROM[l]) * PIECES + q

        def matmul_number(l, lap, s):
            return (lap - MATMUL_FROM[l]) * len(MATMUL_SLOTS) + MATMUL_SLOTS.index(s)

        def chunk_cols(c):
            return slice(c * PER_CHUNK * F, (c + 1) * PER_CHUNK * F)

        @block.sync
        def _(sp):
            for c in range(CHUNKS):
                sp.dma_start(x_sb[:, chunk_cols(c)].rearrange("p (b f) -> p b f", f=F), chunk_of(x_rows, c)
                             ).then_inc(x_loaded[c], 16)
            sp.dma_start(dst_sb[:, :], dst).then_inc(edges_loaded, 16)
            sp.dma_start(base_sb[:, :], window_base.partition_broadcast(P)).then_inc(edges_loaded, 16)
            sp.dma_start(type_sb[:, :], edge_type).then_inc(edges_loaded, 16)
            sp.dma_start(src_sb[:, :], src).then_inc(src_loaded, 16)
            for c in range(CHUNKS):
                sp.wait_ge(rows_by_act, c + 1)
                sp.wait_ge(rows_by_pool, c + 1)
                sp.dma_start(chunk_of(rows[0], c), h_rows[0][:, chunk_cols(c)].rearrange("p (b f) -> p b f", f=F)
                             ).then_inc(rows_stored, 16)

            for k in range(2):
                for piece in range(STAGED_PIECES):
                    cols = slice(piece * STAGED // STAGED_PIECES, (piece + 1) * STAGED // STAGED_PIECES)
                    sp.dma_start(src_staging[k][:, cols],
                                 matmul_src[k * STAGED + cols.start:k * STAGED + cols.stop].partition_broadcast(P)
                                 ).then_inc(src_widened, 16)

            def store(l, fin):
                made, goes = (h_rows[1], rows[1]) if l == 0 else (out_sb, out_rows)
                with sp.Fori(0, LAST) as b:
                    sp.wait_ge(fin["staged"], b + 1)
                    sp.dma_start(goes[ds(b * P, P), :], made[:, ds(b * F, F)]).then_inc(fin["stored"], 16)
                sp.wait_ge(fin["staged"], BLOCKS)
                sp.dma_start(goes[LAST * P:N_NODES, :], made[0:LAST_NODES, LAST * F:]).then_inc(fin["stored"], 16)
                sp.wait_ge(fin["stored"], 16 * BLOCKS)

            for l in range(2):
                store(l, regular_finish[l])
                with if_irregular(sp):
                    store(l, again_finish[l])

        @block.gpsimd
        def _(pool):
            nc.gpsimd.memset(eps[:, :], 1e-5).then_inc(eps_ready, 1)
            nc.gpsimd.iota(numbers[:, :], pattern=[[1, BCOLS]], base=0, channel_multiplier=0,
                           allow_small_or_imprecise_dtypes=True).then_inc(constants_ready, 1)
            first, last = 2 * GROUP, TILES - GROUP
            even = (last - first) // (SLOTS * GROUP)
            nc.gpsimd.memset(finished_below[:, 0:first], 0.0).then_inc(constants_ready, 1)
            nc.gpsimd.iota(finished_below[:, first:first + even * SLOTS * GROUP],
                           pattern=[[P, even], [0, SLOTS * GROUP]], base=0, channel_multiplier=0,
                           allow_small_or_imprecise_dtypes=True).then_inc(constants_ready, 1)
            nc.gpsimd.memset(finished_below[:, first + even * SLOTS * GROUP:last], float(even * P)
                             ).then_inc(constants_ready, 1)
            nc.gpsimd.memset(finished_below[:, last:], float(LAST * P)).then_inc(constants_ready, 1)
            nc.gpsimd.iota(node_id[:, :], pattern=[[P, BLOCKS]], base=0, channel_multiplier=1,
                           allow_small_or_imprecise_dtypes=True).then_inc(constants_ready, 1)
            nc.gpsimd.memset(ones[:, :], 1.0).then_inc(identity_ready, 1)
            nc.gpsimd.memset(identity[:, :], 0.0).then_inc(identity_ready, 1)
            nc.gpsimd.memset(tail_mask[:, :], 1.0).then_inc(identity_ready, 1)
            pool.wait_ge(identity_ready, 3)
            nc.gpsimd.affine_select(out=identity[:, :], in_=identity[:, :], compare_op=ALU.not_equal, fill=1.0,
                                    base=0, pattern=[[-1, P]], channel_multiplier=1).then_inc(identity_ready, 1)
            nc.gpsimd.affine_select(out=tail_mask[:, :], in_=tail_mask[:, :], compare_op=ALU.is_ge, fill=0.0,
                                    base=N_EDGES - 1 - TAIL * P, pattern=[[-P, TILES - TAIL]],
                                    channel_multiplier=-1).then_inc(constants_ready, 1)
            nc.gpsimd.memset(sums[:, 0:CLEAR_BY_POOL], 0.0).then_inc(sums_cleared, 1)
            for c in range(CHUNKS):
                pool.wait_ge(norm_ready, c + 1)
                mine = range(c * PER_CHUNK + BY_ACT[c], (c + 1) * PER_CHUNK)
                for b in mine:
                    shifted = nc.gpsimd.tensor_scalar(h_rows[0][:, b * F:(b + 1) * F], x_sb[:, b * F:(b + 1) * F],
                                                      rstd[:, b:b + 1], shift[:, b:b + 1], ALU.mult, ALU.add)
                shifted.then_inc(rows_shifted, 1)
                pool.wait_ge(rows_shifted, c + 1)
                share = h_rows[0][:, mine[0] * F:(mine[-1] + 1) * F]
                nc.gpsimd.tensor_scalar(share, share, 0.0, None, ALU.max).then_inc(rows_by_pool, 1)
            pool.wait_ge(extremes_ready, 1)
            nc.gpsimd.partition_all_reduce(extremes_all[:, :], extremes[:, :], P,
                                           bass.bass_isa.ReduceOp.max).then_inc(extremes_reduced, 1)

            def gather_tile(l, s, k, done):
                nc.gpsimd.indirect_dma_start(
                    out=gathered[:, s, k, :], out_offset=None, in_=rows[l],
                    in_offset=bass.IndirectOffsetOnAxis(ap=slot_index[:, s, k:k + 1], axis=0)).then_inc(done, 16)

            def gather(l, g, s, lap):
                pool.wait_ge(slot_indexed[l], g + 1)
                pool.sem_inc(gathers_begun, 1)
                for k in range(GROUP - by_matmul(l, lap, s)):
                    gather_tile(l, s, k, rows_gathered[l][s])

            for l in range(2):
                if l == 0:
                    pool.wait_ge(rows_stored, 16 * CHUNKS)
                else:
                    pool.wait_ge(regular_finish[0]["stored"], 16 * BLOCKS)
                    with if_irregular(pool):
                        pool.wait_ge(again_finish[0]["stored"], 16 * BLOCKS)
                for lap in range(MATMUL_FROM[l]):
                    for s in range(SLOTS):
                        gather(l, lap * SLOTS + s, s, lap)
                with pool.Fori(MATMUL_FROM[l], LAPS) as lap:
                    for s in range(SLOTS):
                        gather(l, lap * SLOTS + s, s, lap)
                if l == 0:
                    pool.wait_ge(irregular_ready, 1)
                    nc.gpsimd.partition_all_reduce(irregular_all[:, :], irregular[:, :], P,
                                                   bass.bass_isa.ReduceOp.max).then_inc(irregular_reduced, 1)
                gather(l, GROUPS - 2, 0, LAPS)
                pool.wait_ge(slot_indexed[l], GROUPS)
                for k in range(LAST_TILES):
                    gather_tile(l, 1, k, last_gathered[l][k])
                with if_irregular(pool):
                    with pool.Fori(0, FULL_TILES) as t:
                        pool.wait_ge(edge_indexed, t + l * FULL_TILES + 1)
                        pool.sem_inc(gathers_begun, 1)
                        nc.gpsimd.indirect_dma_start(
                            out=gathered[:, 0, 0, :], out_offset=None, in_=rows[l],
                            in_offset=bass.IndirectOffsetOnAxis(ap=edge_index[:, :], axis=0),
                        ).then_inc(edge_gathered, 16)

        @block.scalar
        def _(act):
            act.dma_start(ew_sb[:, :], edge_weight).then_inc(weights_loaded, 16)
            act.wait_ge(eps_ready, 1)
            for c in range(CHUNKS):
                blocks = slice(c * PER_CHUNK, (c + 1) * PER_CHUNK)
                act.wait_ge(moments_ready, c + 1)
                nc.scalar.activation(rstd[:, blocks], moments[:, blocks, 1], ACT.Sqrt, bias=eps[:, :]
                                     ).then_inc(std_ready, 1)
                act.wait_ge(norm_ready, c + 1)
                for b in range(c * PER_CHUNK, c * PER_CHUNK + BY_ACT[c]):
                    last = nc.scalar.activation(h_rows[0][:, b * F:(b + 1) * F], x_sb[:, b * F:(b + 1) * F], ACT.Relu,
                                                bias=shift[:, b:b + 1], scale=rstd[:, b:b + 1])
                last.then_inc(rows_by_act, 1)

            def place_index(l, g, s):
                nc.scalar.copy(slot_index[:, s, :], src_sb[:, ds(g * GROUP, GROUP)]).then_inc(slot_indexed[l], 1)

            def build_select(l, g, s, tiles):
                for k in tiles:
                    last = nc.scalar.activation(select[:, s, k, :], numbers[:, 0:COLS], ACT.Abs,
                                                bias=key[:, ds(g * GROUP + k, 1)], scale=-1.0)
                last.then_inc(key_distanced[l], 1)
                act.wait_ge(key_distanced[l], g + 1)
                act.sem_inc(act_selects_begun, 1)
                for k in tiles:
                    last = nc.scalar.activation(select[:, s, k, :], select[:, s, k, :], ACT.Relu,
                                                bias=weight[:, ds(g * GROUP + k, 1)],
                                                scale=minus_weight[:, ds(g * GROUP + k, 1)])
                last.then_inc(select_by_act[l], 1)

            def replace_index(l, g, s):
                act.wait_ge(windows_summed[l], g - SLOTS + 1)
                place_index(l, g, s)
                build_select(l, g, s, range(BY_VECTOR, LAST_TILES if is_static(g) and g == GROUPS - 1 else GROUP))

            def take_rows(l, fin, b):
                nc.scalar.copy(block_rows[:, :], h_rows[l][:, ds(b * F, F)]).then_inc(fin["rows_taken"], 1)

            def copy_sums(l, fin, b):
                nc.scalar.copy(block_sums[:, :, :], sums[:, ds(b * BCOLS, BCOLS)].rearrange("p (n r) -> p r n", r=R)
                               ).then_inc(fin["sums_taken"], 1)

            def take_sums(l, fin, b, added):
                act.wait_ge(*added)
                copy_sums(l, fin, b)
                act.wait_ge(fin["sums_taken"], b + 1)
                act.sem_inc(clears_begun, 1)
                if l == 0:
                    nc.scalar.memzero(sums[:, ds(b * BCOLS, BCOLS)]).then_inc(fin["sums_released"], 1)
                else:
                    act.sem_inc(fin["sums_released"], 1)

            def take_cols(l, fin, b):
                act.wait_ge(fin["rows_turned"], b + 1)
                nc.scalar.copy(block_cols[:, :], turned_ps[:, 0:P]).then_inc(fin["cols_taken"], 1)

            def new_block(l, fin, b, product=block_ps):
                act.wait_ge(fin["multiplied"], b + 1)
                if l == 0:
                    nc.scalar.activation(h_rows[1][:, ds(b * F, F)], product[:, 0:F], ACT.Relu
                                         ).then_inc(fin["staged"], 1)
                    act.wait_ge(fin["staged"], b + 1)
                    act.sem_inc(parts_begun, 1)
                    nc.scalar.copy(parts[1][:, ds(b, 1), 0, :], h_rows[1][:, None, ds(b * F, F)]
                                   ).then_inc(first_part_made, 1)

            act.wait_ge(src_loaded, 16)
            for s in range(SLOTS):
                place_index(0, s, s)
            nc.scalar.memzero(sums[:, CLEAR_BY_POOL:CLEAR_BY_ACT]).then_inc(sums_cleared, 1)
            for l, (w, root, b) in enumerate(((W1, root1, b1), (W2, root2, b2))):
                act.dma_start(W_sb[l][:, :], w).then_inc(params_loaded, 16)
                act.dma_start(root_sb[l][:, :], root).then_inc(params_loaded, 16)
                act.dma_start(b_sb[l][:, :], b).then_inc(params_loaded, 16)
            act.wait_ge(weights_ready, 1)
            for s in range(SLOTS):
                build_select(0, s, s, range(BY_VECTOR, GROUP))
            act.wait_ge(rows_by_pool, CHUNKS)
            act.wait_ge(rows_by_act, CHUNKS)
            nc.scalar.copy(parts[0][:, :, 0, :], h_rows[0][:, :].rearrange("p (b f) -> p b f", f=F)
                           ).then_inc(first_parts, 1)
            act.wait_ge(constants_ready, 7)
            nc.scalar.copy(node_table[:, :, :], node_id[:, :, None].to_broadcast([P, BLOCKS, P])
                           ).then_inc(tables_ready, 1)
            act.wait_ge(src_widened, 2 * STAGED_PIECES * 16)
            for k in range(2):
                nc.scalar.copy(src_wide[:, k * STAGED:(k + 1) * STAGED], src_staging[k][:, 0:STAGED]
                               ).then_inc(tables_ready, 1)
            for l in range(2):
                fin = regular_finish[l]
                if l == 1:
                    for s in range(SLOTS):
                        build_select(l, s, s, range(BY_VECTOR, GROUP))
                for s in range(SLOTS):
                    replace_index(l, SLOTS + s, s)
                with act.Fori(2, LAPS) as lap:
                    b = lap - 2
                    replace_index(l, lap * SLOTS, 0)
                    take_rows(l, fin, b)
                    replace_index(l, lap * SLOTS + 1, 1)
                    take_cols(l, fin, b)
                    take_sums(l, fin, b, (window_added[l], ((lap - 1) * SLOTS + 2) * PER))
                    replace_index(l, lap * SLOTS + 2, 2)
                    new_block(l, fin, b)
                    replace_index(l, lap * SLOTS + 3, 3)
                replace_index(l, GROUPS - 2, 0)
                take_rows(l, fin, LAST - 2)
                replace_index(l, GROUPS - 1, 1)
                take_cols(l, fin, LAST - 2)
                take_sums(l, fin, LAST - 2, (window_added[l], ((LAPS - 1) * SLOTS + 2) * PER))
                act.wait_ge(last_turned, l + 1)
                nc.scalar.copy(last_cols[:, :, :], other_block_ps[:, P:3 * P].rearrange("p (k n) -> p k n", n=P)
                               ).then_inc(last_cols_taken, 1)
                new_block(l, fin, LAST - 2)
                act.wait_ge(window_added[l], (GROUPS - 1) * PER)
                copy_sums(l, fin, LAST - 1)
                if l == 0:
                    act.wait_ge(windows_summed[0], GROUPS)
                    for s in range(SLOTS):
                        place_index(1, s, s)
                new_block(l, fin, LAST - 1, other_block_ps)
                new_block(l, fin, LAST, turned_ps)
                if l == 0:
                    act.wait_ge(window_added[0], WINDOWS)
                    nc.scalar.memzero(sums[:, (LAST - 1) * BCOLS:]).then_inc(last_sums_cleared, 1)
                with if_irregular(act):
                    fin = again_finish[l]
                    with act.Fori(0, BLOCKS) as b:
                        take_rows(l, fin, b)
                        take_cols(l, fin, b)
                        take_sums(l, fin, b, (edge_added, (l + 1) * FULL_TILES * BLOCKS))
                        new_block(l, fin, b)

        @block.vector
        def _(dve):
            steps = [0]

            def link(instruction):
                steps[0] += 1
                instruction.then_inc(dve_step, 1)
                dve.wait_ge(dve_step, steps[0])

            def chunk_moments(c):
                blocks = range(c * PER_CHUNK, (c + 1) * PER_CHUNK)
                dve.wait_ge(x_loaded[c], 16)
                for b in blocks:
                    last = nc.vector.bn_stats(stats[:, b, :], x_sb[:, b * F:(b + 1) * F])
                last.then_inc(stats_ready, 1)
                dve.wait_ge(stats_ready, c + 1)
                for b in blocks:
                    last = nc.vector.bn_aggr(moments[:, b, :], stats[:, b, :])
                last.then_inc(moments_ready, 1)

            def chunk_norm(c):
                blocks = slice(c * PER_CHUNK, (c + 1) * PER_CHUNK)
                dve.wait_ge(std_ready, c + 1)
                nc.vector.reciprocal(rstd[:, blocks], rstd[:, blocks]).then_inc(rstd_ready, 1)
                dve.wait_ge(rstd_ready, c + 1)
                nc.vector.scalar_tensor_tensor(out=shift[:, blocks], in0=moments[:, blocks, 0], scalar=-1.0,
                                               in1=rstd[:, blocks], op0=ALU.mult, op1=ALU.mult
                                               ).then_inc(norm_ready, 1)

            def by_window(a):
                return a[:, :].rearrange("p (w k) -> p w k", k=PAIR)

            def edge_weights():
                dve.wait_ge(extremes_reduced, 1)
                link(nc.vector.tensor_scalar(ew_range[:, 0:1], extremes_all[:, 0:1], extremes_all[:, 1:2], 1e-8,
                                             ALU.add, ALU.add))
                link(nc.vector.reciprocal(ew_range[:, 1:2], ew_range[:, 0:1]))
                link(nc.vector.tensor_scalar(weight[:, :], ew_sb[:, :], extremes_all[:, 1:2], ew_range[:, 1:2],
                                             ALU.add, ALU.mult))
                dve.wait_ge(constants_ready, 7)
                link(nc.vector.tensor_tensor(weight[:, TAIL:], weight[:, TAIL:], tail_mask[:, :], ALU.mult))
                nc.vector.tensor_scalar(minus_weight[:, :], weight[:, :], -1.0, None, ALU.mult
                                        ).then_inc(weights_ready, 1)

            def edge_keys():
                dve.wait_ge(edges_loaded, 48)
                link(nc.vector.tensor_scalar(first_col[:, :], base_sb[:, :], float(R), None, ALU.mult))
                pair = base_sb[:, :].rearrange("p (g j) -> p g j", j=PER)
                link(nc.vector.scalar_tensor_tensor(out=first_nodes[:, :], in0=pair[:, :, 1], scalar=float(NODE_UNIT),
                                                    in1=pair[:, :, 0], op0=ALU.mult, op1=ALU.add))
                link(nc.vector.scalar_tensor_tensor(out=column[:, :], in0=dst_sb[:, :], scalar=float(R),
                                                    in1=type_sb[:, :], op0=ALU.mult, op1=ALU.add))
                link(nc.vector.tensor_tensor(by_window(key), by_window(column),
                                             first_col[:, :, None].to_broadcast([P, WINDOWS, PAIR]), ALU.subtract))

            def edge_regularity():
                link(nc.vector.tensor_scalar(inside[:, :], key[:, :], 0.0, None, ALU.is_ge))
                link(nc.vector.scalar_tensor_tensor(out=inside[:, :], in0=key[:, :], scalar=float(COLS),
                                                    in1=inside[:, :], op0=ALU.is_lt, op1=ALU.mult))
                link(nc.vector.tensor_tensor(regular[:, :], dst_sb[:, :], finished_below[:, :], ALU.is_ge))
                link(nc.vector.tensor_tensor(regular[:, :], regular[:, :], inside[:, :], ALU.mult))
                link(nc.vector.tensor_reduce(out=least_regular[:, :], in_=regular[:, :], axis=AX.X, op=ALU.min))
                nc.vector.tensor_scalar(irregular[:, :], least_regular[:, :], -1.0, 1.0, ALU.mult, ALU.add
                                        ).then_inc(irregular_ready, 1)

            def build_select(l, g, s, tiles=BY_VECTOR):
                for k in range(tiles):
                    t = g * GROUP + k
                    last = nc.vector.tensor_scalar(select[:, s, k, :], window_numbers,
                                                   key[:, ds(t, 1)], weight[:, ds(t, 1)], ALU.is_equal, ALU.mult)
                last.then_inc(select_ready[l], 1)

            def window_cols(g):
                both = dve.value_load(first_nodes[0:1, ds(g, 1)], min_val=0, max_val=NODE_UNIT * N_NODES - 1)
                return [R * (both % NODE_UNIT), R * (both // NODE_UNIT)]

            def add_windows(l, g, s, cols=None):
                if cols is None:
                    cols = window_cols(g)
                dve.wait_ge(windows_summed[l], g + 1)
                for j in range(PER):
                    if not is_static(g) or g * PER + j > 0:
                        dve.wait_ge(window_added[l], g * PER + j)
                    nc.vector.tensor_tensor(sums[:, ds(cols[j], COLS)], sums[:, ds(cols[j], COLS)],
                                            window_ps[s % 2][:, j * COLS:(j + 1) * COLS],
                                            ALU.add).then_inc(window_added[l], 1)

            def sums_released(l, fin, b):
                dve.wait_ge(fin["sums_released"], b + 1)

            def build_piece(l, lap, q):
                before = piece_number(l, lap, q) - len(HALVES)
                if not is_static(before) or before >= 0:
                    dve.wait_ge(matmul_gathered[l], before + 1)
                k, blocks = q // len(HALVES), HALVES[q % len(HALVES)]
                tile = lap * len(MATMUL_SLOTS) + k
                nc.vector.tensor_tensor(source_onehot[:, blocks, :],
                                        src_wide[:, None, ds(tile * P, P)
                                                 ].to_broadcast([P, blocks.stop - blocks.start, P]),
                                        node_table[:, blocks, :], ALU.is_equal).then_inc(onehot_ready[l], 1)

            def join_parts(l, lap, s):
                dve.wait_ge(matmul_gathered[l], (matmul_number(l, lap, s) + 1) * len(HALVES))
                if not is_static(lap) or lap > 0:
                    dve.wait_ge(windows_summed[l], (lap - 1) * SLOTS + s + 1)
                products = gather_ps[MATMUL_SLOTS.index(s)][:, 0:PARTS * F].rearrange("p (q f) -> p f q", f=F)
                nc.vector.tensor_reduce(out=gathered[:, s, GROUP - 1, :], in_=products, axis=AX.X,
                                        op=ALU.add).then_inc(matmul_rows_ready[l], 1)

            def split(l, b, count, done, n):
                h = h_rows[l][:, ds(b * F, count * F)].rearrange("p (b f) -> p b f", f=F)
                left = rest[:, 0:count * F].rearrange("p (b f) -> p b f", f=F)
                part = [parts[l][:, ds(b, count), q, :] for q in range(PARTS)]
                nc.vector.tensor_tensor(left, h, part[0], ALU.subtract)
                nc.vector.tensor_tensor(part[1], h, part[0], ALU.subtract).then_inc(done, 1)
                dve.wait_ge(done, n + 1)
                nc.vector.tensor_tensor(part[2], left, part[1], ALU.subtract).then_inc(done, 1)
                dve.wait_ge(done, n + 2)

            def result_block(l, fin, b, product=block_ps):
                dve.wait_ge(fin["multiplied"], b + 1)
                if l == 1:
                    nc.vector.tensor_tensor(out_sb[:, ds(b * F, F)], product[:, 0:F], x_sb[:, ds(b * F, F)], ALU.add
                                            ).then_inc(fin["staged"], 1)

            def every_edge(l):
                nc.vector.memset(sums[:, :], 0.0).then_inc(sums_wiped, 1)
                dve.wait_ge(sums_wiped, l + 1)
                with dve.Fori(0, FULL_TILES) as t:
                    done = (t + l * FULL_TILES) * BLOCKS
                    nc.vector.tensor_copy(edge_index[:, :], src_sb[:, ds(t, 1)]).then_inc(edge_indexed, 1)
                    nc.vector.tensor_copy(edge_key[:, :], column[:, ds(t, 1)]).then_inc(edge_moved, 1)
                    with dve.Fori(0, BLOCKS) as b:
                        dve.wait_ge(edge_moved, done + t + l * FULL_TILES + b + 1)
                        nc.vector.tensor_scalar(edge_select[:, :], numbers[:, :], edge_key[:, :],
                                                weight[:, ds(t, 1)], ALU.is_equal, ALU.mult
                                                ).then_inc(edge_selected, 1)
                        dve.wait_ge(edge_selected, done + b + 1)
                        nc.vector.tensor_scalar(edge_key[:, :], edge_key[:, :], -float(BCOLS), None,
                                                ALU.add).then_inc(edge_moved, 1)
                        dve.wait_ge(edge_summed, done + b + 1)
                        nc.vector.tensor_tensor(sums[:, ds(b * BCOLS, BCOLS)], sums[:, ds(b * BCOLS, BCOLS)],
                                                edge_ps[:, :], ALU.add).then_inc(edge_added, 1)
                        dve.wait_ge(edge_added, done + b + 1)

            for c in range(CHUNKS):
                chunk_moments(c)
                if c:
                    chunk_norm(c - 1)
            chunk_norm(CHUNKS - 1)
            dve.wait_ge(weights_loaded, 16)
            nc.vector.tensor_reduce(out=extremes[:, 0:1], in_=ew_sb[:, :], axis=AX.X, op=ALU.max)
            nc.vector.tensor_reduce(out=extremes[:, 1:2], in_=ew_sb[:, :], axis=AX.X, op=ALU.min, negate=True
                                    ).then_inc(extremes_ready, 1)
            edge_keys()
            edge_weights()
            nc.vector.tensor_copy(window_numbers, numbers[:, 0:COLS]).then_inc(constants_placed, 1)
            dve.wait_ge(constants_placed, 1)

            for l in range(2):
                fin = regular_finish[l]
                if l == 1:
                    dve.wait_ge(first_part_made, BLOCKS)
                    split(1, SPLIT_LATER, BLOCKS - SPLIT_LATER, parts_split[1], 2 * SPLIT_LATER)
                if MATMUL_FROM[l] == 0:
                    for q in range(2):
                        build_piece(l, 0, q)
                for g in range(SLOTS):
                    build_select(l, g, g)
                if l == 0:
                    nc.vector.memset(sums[:, CLEAR_BY_ACT:], 0.0).then_inc(sums_cleared, 1)
                    dve.wait_ge(sums_cleared, 3)
                else:
                    dve.wait_ge(regular_finish[0]["sums_released"], LAST - 1)
                    dve.wait_ge(last_sums_cleared, 1)

                if MATMUL_FROM[l] == 0:
                    build_piece(l, 0, 2)

                def lap_of_groups(lap):
                    b = lap - 1
                    started = not is_static(lap) or lap > 0
                    for s in range(SLOTS):
                        g = lap * SLOTS + s
                        if by_matmul(l, lap, s + 1):
                            join_parts(l, lap, s + 1)
                        add_windows(l, g, s, ahead.get(g) if is_static(g) else None)
                        if s == 3 and started:
                            result_block(l, fin, b)
                        if s == 2 and l == 0 and (not is_static(lap) or 1 < lap < LAPS - 1):
                            dve.wait_ge(first_part_made, b)
                            split(1, b - 1, 1, parts_split[1], 2 * (b - 1))
                        if l == 0 and is_static(lap) and 1 <= g <= CHUNKS:
                            dve.wait_ge(first_parts, 1)
                            split(0, (g - 1) * PER_CHUNK, PER_CHUNK, parts_split[0], 2 * (g - 1))
                        piece_lap, q = (lap, 3) if s == 0 else (lap + 1, s - 1)
                        if matmul_lap(l, piece_lap):
                            if l == 0 and is_static(piece_lap) and piece_lap == MATMUL_FROM[0] and q == 0:
                                dve.wait_ge(tables_ready, 3)
                            build_piece(l, piece_lap, q)
                        if not is_static(g) or g + SLOTS < GROUPS:
                            build_select(l, g + SLOTS, s)
                        if l == 0 and is_static(lap) and lap == 1 and s == 3:
                            edge_regularity()
                        if s == 1 and started:
                            sums_released(l, fin, b)
                        if is_static(g) and GROUPS - 6 <= g < GROUPS - 4:
                            ahead[g + 4] = window_cols(g + 4)

                ahead = {}
                lap_of_groups(0)
                lap_of_groups(1)
                with dve.Fori(2, LAPS - 1) as lap:
                    lap_of_groups(lap)
                lap_of_groups(LAPS - 1)
                add_windows(l, GROUPS - 2, 0, ahead[GROUPS - 2])
                dve.wait_ge(fin["sums_taken"], LAST)
                add_windows(l, GROUPS - 1, 1, ahead[GROUPS - 1])
                if l == 0:
                    dve.wait_ge(irregular_reduced, 1)
                    nc.vector.tensor_copy(irregular_flag[:, :], irregular_all[:, :]).then_inc(flag_ready, 1)
                result_block(l, fin, LAST - 1, other_block_ps)
                result_block(l, fin, LAST, turned_ps)
                with if_irregular(dve):
                    dve.wait_ge(fin["stored"], 16 * BLOCKS)
                    if l == 0:
                        dve.wait_ge(last_sums_cleared, 1)
                    every_edge(l)
                    fin = again_finish[l]
                    with dve.Fori(0, BLOCKS) as b:
                        result_block(l, fin, b)
                        if l == 0:
                            dve.wait_ge(first_part_made, BLOCKS + b + 1)
                            split(1, b, 1, parts_again, 2 * b)
                    if l == 0:
                        dve.wait_ge(fin["sums_released"], BLOCKS)

        @block.tensor
        def _(pe):
            pe.wait_ge(identity_ready, 4)

            def sum_window(s, k, last_tile):
                j = k // PAIR
                return nc.tensor.matmul(window_ps[s % 2][:, j * COLS:(j + 1) * COLS], gathered[:, s, k, :],
                                        select[:, s, k, :], start=(k % PAIR == 0),
                                        stop=(k % PAIR == PAIR - 1 or k == last_tile))

            def selects_built(l, g):
                pe.wait_ge(select_ready[l], g + 1)
                pe.wait_ge(select_by_act[l], g + 1)
                if not is_static(g) or g >= 2:
                    pe.wait_ge(window_added[l], (g - 1) * PER)

            def sum_group(l, g, s, turn):
                selects_built(l, g)
                if by_matmul(l, turn, s):
                    pe.wait_ge(rows_gathered[l][s], 16 * ((GROUP - 1) * (turn + 1) + MATMUL_FROM[l]))
                    pe.wait_ge(matmul_rows_ready[l], matmul_number(l, turn, s) + 1)
                else:
                    pe.wait_ge(rows_gathered[l][s], 16 * GROUP * (turn + 1))
                for k in range(GROUP):
                    last = sum_window(s, k, GROUP - 1)
                last.then_inc(windows_summed[l], 1)

            def gather_piece(l, lap, q):
                pe.wait_ge(onehot_ready[l], piece_number(l, lap, q) + 1)
                for b in range(BLOCKS)[HALVES[q % len(HALVES)]]:
                    last = nc.tensor.matmul(gather_ps[q // len(HALVES)][:, 0:PARTS * F], source_onehot[:, b, :],
                                            parts[l][:, b, :, :].rearrange("p q f -> p (q f)"),
                                            start=(b == 0), stop=(b == BLOCKS - 1))
                last.then_inc(matmul_gathered[l], 1)

            def sum_last_window(l):
                selects_built(l, GROUPS - 1)
                for k in range(LAST_TILES):
                    pe.wait_ge(last_gathered[l][k], 16)
                    last = sum_window(1, k, LAST_TILES - 1)
                last.then_inc(windows_summed[l], 1)

            def turn_rows(l, fin, b):
                pe.wait_ge(fin["rows_taken"], b + 1)
                nc.tensor.transpose(turned_ps[:, 0:P], block_rows[:, :], identity[:, :]
                                    ).then_inc(fin["rows_turned"], 1)

            def bias_and_root(l, fin, b, product=block_ps):
                nc.tensor.matmul(product[:, 0:F], ones[:, :], b_sb[l][:, :], start=True, stop=False)
                pe.wait_ge(fin["cols_taken"], b + 1)
                nc.tensor.matmul(product[:, 0:F], block_cols[:, :], root_sb[l][:, :], start=False, stop=False
                                 ).then_inc(fin["rooted"], 1)

            def turn_last_rows(l):
                for k in range(2):
                    last = nc.tensor.transpose(other_block_ps[:, (k + 1) * P:(k + 2) * P],
                                               h_rows[l][:, (LAST - 1 + k) * F:(LAST + k) * F], identity[:, :])
                last.then_inc(last_turned, 1)

            def last_bias_and_root(l):
                pe.wait_ge(last_cols_taken, l + 1)
                for k, product in enumerate((other_block_ps, turned_ps)):
                    nc.tensor.matmul(product[:, 0:F], ones[:, :], b_sb[l][:, :], start=True, stop=False)
                    nc.tensor.matmul(product[:, 0:F], last_cols[:, k, :], root_sb[l][:, :], start=False, stop=False)

            def relations(l, fin, b, product=block_ps, block_sums=block_sums):
                for r in range(R):
                    last = nc.tensor.matmul(product[:, 0:F], block_sums[:, r, :], W_sb[l][:, r * F:(r + 1) * F],
                                            start=False, stop=(r == R - 1))
                last.then_inc(fin["multiplied"], 1)

            def multiply_block(l, fin, b):
                bias_and_root(l, fin, b)
                pe.wait_ge(fin["sums_taken"], b + 1)
                relations(l, fin, b)

            def staged(l, fin, b):
                pe.wait_ge(fin["staged"], b + 1)

            for l in range(2):
                fin = regular_finish[l]

                def piece(lap, q):
                    if not matmul_lap(l, lap):
                        return
                    if is_static(lap) and lap == MATMUL_FROM[l] and q == 0:
                        pe.wait_ge(parts_split[l], 2 * (CHUNKS if l == 0 else SPLIT_LATER + 1))
                        if l == 1:
                            with if_irregular(pe):
                                pe.wait_ge(parts_again, 2 * BLOCKS)
                    gather_piece(l, lap, q)

                def lap_of_groups(lap):
                    b = lap - 1
                    last = is_static(lap) and lap == LAPS - 1
                    started = not is_static(lap) or lap > 0
                    sum_group(l, lap * SLOTS, 0, lap)
                    piece(lap, 2)
                    if started:
                        turn_rows(l, fin, b)
                    if last:
                        turn_last_rows(l)
                    sum_group(l, lap * SLOTS + 1, 1, lap)
                    piece(lap, 3)
                    sum_group(l, lap * SLOTS + 2, 2, lap)
                    piece(lap + 1, 0)
                    if not is_static(lap) or lap > 1:
                        staged(l, fin, b - 1)
                    if started:
                        multiply_block(l, fin, b)
                    if last:
                        last_bias_and_root(l)
                    sum_group(l, lap * SLOTS + 3, 3, lap)
                    piece(lap + 1, 1)

                for q in range(2):
                    piece(0, q)
                lap_of_groups(0)
                pe.wait_ge(params_loaded, 96)
                lap_of_groups(1)
                with pe.Fori(2, LAPS - 1) as lap:
                    lap_of_groups(lap)
                lap_of_groups(LAPS - 1)
                sum_group(l, GROUPS - 2, 0, LAPS)
                sum_last_window(l)
                pe.wait_ge(fin["sums_taken"], LAST)
                relations(l, fin, LAST - 1, other_block_ps)
                pe.wait_ge(window_added[l], WINDOWS)
                relations(l, fin, LAST, turned_ps,
                          sums[:, LAST * BCOLS:].rearrange("p (n r) -> p r n", r=R))
                with if_irregular(pe):
                    staged(l, fin, BLOCKS - 1)
                    with pe.Fori(0, FULL_TILES) as t:
                        done = (t + l * FULL_TILES) * BLOCKS
                        with pe.Fori(0, BLOCKS) as b:
                            pe.wait_ge(edge_gathered, (t + l * FULL_TILES + 1) * 16)
                            pe.wait_ge(edge_selected, done + b + 1)
                            nc.tensor.matmul(edge_ps[:, :], gathered[:, 0, 0, :], edge_select[:, :],
                                             start=True, stop=True).then_inc(edge_summed, 1)
                    fin = again_finish[l]
                    with pe.Fori(0, BLOCKS) as b:
                        turn_rows(l, fin, b)
                        multiply_block(l, fin, b)
                        staged(l, fin, b)


def kernel(x, src, dst, edge_type_4, edge_weight, L0_gnn_W1, L0_gnn_root1, L0_gnn_b1,
           L0_gnn_W2, L0_gnn_root2, L0_gnn_b2):
    import numpy as np
    import concourse.bacc as bacc
    from concourse.bass_utils import run_bass_kernel_spmd

    def by_tile(a):
        return np.ascontiguousarray(np.pad(np.asarray(a), (0, TILES * P - N_EDGES), mode="edge").reshape(TILES, P).T)

    def relations_side_by_side(w):
        return np.ascontiguousarray(np.asarray(w).transpose(1, 0, 2).reshape(F, R * F))

    x_padded = np.pad(np.asarray(x), ((0, NODES - N_NODES), (0, 0)))
    dst_tiles = by_tile(dst)
    arrays = {
        "x_rows": x_padded,
        "src": by_tile(src),
        "matmul_src": np.ascontiguousarray(by_tile(src)[:, MATMUL_TILES].T).reshape(-1),
        "dst": dst_tiles,
        "window_base": np.ascontiguousarray(dst_tiles[0, ::PAIR]),
        "edge_type": by_tile(edge_type_4),
        "edge_weight": by_tile(edge_weight),
        "W1": relations_side_by_side(L0_gnn_W1),
        "root1": np.asarray(L0_gnn_root1),
        "b1": np.asarray(L0_gnn_b1).reshape(1, F),
        "W2": relations_side_by_side(L0_gnn_W2),
        "root2": np.asarray(L0_gnn_root2),
        "b2": np.asarray(L0_gnn_b2).reshape(1, F),
    }
    nc = bacc.Bacc("TRN2", target_bir_lowering=False, num_devices=1)
    args = [nc.dram_tensor(name, a.shape, mybir.dt.from_np(a.dtype), kind="ExternalInput").ap()
            for name, a in arrays.items()]
    out = nc.dram_tensor("out_rows", (N_NODES, F), mybir.dt.float32, kind="ExternalOutput").ap()
    gnn_kernel(nc, *args, out)
    result = run_bass_kernel_spmd(nc, [arrays], core_ids=[0])
    return result.results[0]["out_rows"]
```
